# Optimizing a Trainium2 kernel written in Bass

```python
import numpy as np
import jax
import jax.numpy as jnp

def _softmax(x, axis=-1):
    return jax.nn.softmax(x, axis=axis)

def _gelu(x):
    return jax.nn.gelu(x, approximate=True)

def _silu(x):
    return jax.nn.silu(x)

def _sigmoid(x):
    return jax.nn.sigmoid(x)

def _layernorm(x, axis=-1, eps=1e-05):
    m = jnp.mean(x, axis=axis, keepdims=True)
    v = jnp.var(x, axis=axis, keepdims=True)
    return (x - m) / jnp.sqrt(v + eps)

def _scatter_add(tgt, idx, src, axis=0):
    return tgt.at[idx].add(src)

def _segment_sum(src, seg, n):
    return jax.ops.segment_sum(src, seg, n)
kernel_name = 'mk_gnn_resnorm_d4_gnn_r64_417471'

def setup_inputs(seed: int=0):
    np.random.seed(seed)
    _w = jnp.asarray

    def _rec_inputs():
        import jax
        import jax.numpy as jnp
        _gk = jax.random.key(seed)
        x = -0.0001126 + 1 * jax.random.normal(jax.random.fold_in(_gk, 1), (10000, 768), jnp.float32)
        _s = jax.random.randint(jax.random.fold_in(_gk, 2), (1250,), 0, 10000, jnp.int32)
        _d = jax.random.randint(jax.random.fold_in(_gk, 3), (1250,), 0, 10000, jnp.int32)
        _loop = jnp.arange(10000, dtype=jnp.int32)
        src = jnp.concatenate([_s, _d, _loop])
        dst = jnp.concatenate([_d, _s, _loop])
        _o = jnp.argsort(dst, stable=True)
        src = src[_o]
        dst = dst[_o]
        return (x, src, dst)
    x, src, dst = _rec_inputs()

    def _L0_gnn_setup():
        import jax, jax.numpy as jnp
        import numpy as np
        N = 10000
        E = 2500
        D = 768
        H1, C1 = (4, 192)
        H2, C2 = (2, 96)
        EPS = 1e-05
        NEG_SLOPE = 0.2

        def layer_norm(x, g, b):
            mu = x.mean(-1, keepdims=True)
            var = ((x - mu) ** 2).mean(-1, keepdims=True)
            return (x - mu) * jax.lax.rsqrt(var + EPS) * g + b

        def gat_conv(x, src, dst, W, a_src, a_dst, bias, H, C, n):
            h = (x @ W).reshape(n, H, C)
            s_src = (h * a_src).sum(-1)
            s_dst = (h * a_dst).sum(-1)
            e = jax.nn.leaky_relu(s_src[src] + s_dst[dst], NEG_SLOPE)
            emax = jax.ops.segment_max(e, dst, num_segments=n)
            ee = jnp.exp(e - emax[dst])
            denom = jax.ops.segment_sum(ee, dst, num_segments=n)
            alpha = ee / denom[dst]
            out = jax.ops.segment_sum(alpha[:, :, None] * h[src], dst, num_segments=n)
            return out.reshape(n, H * C) + bias
        key = jax.random.key(seed)
        ks = jax.random.split(key, 16)
        sd = 1.0 / np.sqrt(D)
        inp = {'x': jax.random.normal(ks[0], (N, D), jnp.float32), 'edge_index': jax.random.randint(ks[1], (2, E), 0, N, jnp.int64), 'norm_g': jnp.ones((D,), jnp.float32), 'norm_b': jnp.zeros((D,), jnp.float32), 'W1': jax.random.normal(ks[2], (D, H1 * C1), jnp.float32) * sd, 'a_src1': jax.random.normal(ks[3], (H1, C1), jnp.float32) * sd, 'a_dst1': jax.random.normal(ks[4], (H1, C1), jnp.float32) * sd, 'b1': jnp.zeros((H1 * C1,), jnp.float32), 'W2': jax.random.normal(ks[5], (H1 * C1, H2 * C2), jnp.float32) * sd, 'a_src2': jax.random.normal(ks[6], (H2, C2), jnp.float32) * sd, 'a_dst2': jax.random.normal(ks[7], (H2, C2), jnp.float32) * sd, 'b2': jnp.zeros((H2 * C2,), jnp.float32), 'Wu': jax.random.normal(ks[8], (D + H2 * C2, D), jnp.float32) / np.sqrt(D + H2 * C2), 'bu': jnp.zeros((D,), jnp.float32)}
        return inp
    _L0_gnn_all = _L0_gnn_setup()
    _L0_gnn_in = {k: v for k, v in _L0_gnn_all.items() if k in ('norm_g', 'norm_b', 'W1', 'a_src1', 'a_dst1', 'b1', 'W2', 'a_src2', 'a_dst2', 'b2', 'Wu', 'bu')}
    del _L0_gnn_all

    def _L1_gnn_setup():
        import jax, jax.numpy as jnp
        import numpy as np
        N = 50000
        E = 250000
        H = 12
        D = 64
        NEG_SLOPE = 0.2
        key = jax.random.key(seed)
        k1, k2, k3, k4, k5, k6, k7 = jax.random.split(key, 7)
        h = jax.random.normal(k1, (N, H * D), dtype=jnp.float32)
        src = jnp.concatenate([jnp.arange(N, dtype=jnp.int32), jax.random.randint(k2, (E - N,), 0, N, dtype=jnp.int32)])
        dst = jnp.concatenate([jnp.arange(N, dtype=jnp.int32), jax.random.randint(k3, (E - N,), 0, N, dtype=jnp.int32)])
        xav = 1.414 / np.sqrt(D)
        W_fc = jax.random.normal(k4, (D, D), dtype=jnp.float32) * xav
        attn_l = jax.random.normal(k5, (H, D), dtype=jnp.float32) * 0.15
        attn_r = jax.random.normal(k6, (H, D), dtype=jnp.float32) * 0.15
        W_res = jax.random.normal(k7, (D, D), dtype=jnp.float32) * xav
        return {'h': h, 'W_fc': W_fc, 'attn_l': attn_l, 'attn_r': attn_r, 'W_res': W_res, 'src': src, 'dst': dst}
    _L1_gnn_all = _L1_gnn_setup()
    _L1_gnn_in = {k: v for k, v in _L1_gnn_all.items() if k in ('W_fc', 'attn_l', 'attn_r', 'W_res')}
    del _L1_gnn_all

    def _L2_gnn_setup():
        import jax, jax.numpy as jnp
        import numpy as np
        N_NODES = 10000
        N_EDGES = 100000
        DIM = 768
        key = jax.random.key(seed)
        k1, k2, k3, k4 = jax.random.split(key, 4)
        x = jax.random.normal(k1, (N_NODES, DIM), dtype=jnp.float32)
        edge_index = jax.random.randint(k2, (2, N_EDGES), 0, N_NODES, dtype=jnp.int32)
        W = jax.random.normal(k3, (DIM, DIM), dtype=jnp.float32) / np.sqrt(DIM)
        b = jnp.zeros((DIM,), dtype=jnp.float32)
        return {'x': x, 'edge_index': edge_index, 'W': W, 'b': b}
    _L2_gnn_all = _L2_gnn_setup()
    _L2_gnn_in = {k: v for k, v in _L2_gnn_all.items() if k in ('W', 'b')}
    del _L2_gnn_all

    def _L3_gnn_setup():
        import jax, jax.numpy as jnp
        import numpy as np
        N_NODES = 10000
        D = 768
        N_EDGES = 2500

        def gcn_conv(x, W, b, src, dst, n_nodes):
            h = x @ W
            deg = jax.ops.segment_sum(jnp.ones_like(dst, dtype=h.dtype), dst, num_segments=n_nodes)
            dinv = jnp.where(deg > 0, jax.lax.rsqrt(deg), 0.0)
            norm = dinv[src] * dinv[dst]
            msgs = h[src] * norm[:, None]
            out = jax.ops.segment_sum(msgs, dst, num_segments=n_nodes)
            return out + b

        def add_self_loops(edge_index, n_nodes):
            loop = jnp.arange(n_nodes, dtype=edge_index.dtype)
            src = jnp.concatenate([edge_index[0], loop])
            dst = jnp.concatenate([edge_index[1], loop])
            return (src, dst)
        key = jax.random.key(seed)
        k1, k2, k3, k4 = jax.random.split(key, 4)
        x = jax.random.normal(k1, (N_NODES, D), dtype=jnp.float32)
        edge_index = jax.random.randint(k2, (2, N_EDGES), 0, N_NODES, dtype=jnp.int32)
        glorot = float(np.sqrt(6.0 / (D + D)))
        W1 = jax.random.uniform(k3, (D, D), jnp.float32, -glorot, glorot)
        W2 = jax.random.uniform(k4, (D, D), jnp.float32, -glorot, glorot)
        b1 = jnp.zeros((D,), jnp.float32)
        b2 = jnp.zeros((D,), jnp.float32)
        return {'x': x, 'W1': W1, 'b1': b1, 'W2': W2, 'b2': b2, 'edge_index': edge_index}
    _L3_gnn_all = _L3_gnn_setup()
    _L3_gnn_in = {k: v for k, v in _L3_gnn_all.items() if k in ('W1', 'b1', 'W2', 'b2')}
    del _L3_gnn_all
    return {'x': x, 'src': src, 'dst': dst, 'L0_gnn_norm_g': _L0_gnn_in['norm_g'], 'L0_gnn_norm_b': _L0_gnn_in['norm_b'], 'L0_gnn_W1': _L0_gnn_in['W1'], 'L0_gnn_a_src1': _L0_gnn_in['a_src1'], 'L0_gnn_a_dst1': _L0_gnn_in['a_dst1'], 'L0_gnn_b1': _L0_gnn_in['b1'], 'L0_gnn_W2': _L0_gnn_in['W2'], 'L0_gnn_a_src2': _L0_gnn_in['a_src2'], 'L0_gnn_a_dst2': _L0_gnn_in['a_dst2'], 'L0_gnn_b2': _L0_gnn_in['b2'], 'L0_gnn_Wu': _L0_gnn_in['Wu'], 'L0_gnn_bu': _L0_gnn_in['bu'], 'L1_gnn_W_fc': _L1_gnn_in['W_fc'], 'L1_gnn_attn_l': _L1_gnn_in['attn_l'], 'L1_gnn_attn_r': _L1_gnn_in['attn_r'], 'L1_gnn_W_res': _L1_gnn_in['W_res'], 'L2_gnn_W': _L2_gnn_in['W'], 'L2_gnn_b': _L2_gnn_in['b'], 'L3_gnn_W1': _L3_gnn_in['W1'], 'L3_gnn_b1': _L3_gnn_in['b1'], 'L3_gnn_W2': _L3_gnn_in['W2'], 'L3_gnn_b2': _L3_gnn_in['b2']}

def reference(x, src, dst, L0_gnn_norm_g, L0_gnn_norm_b, L0_gnn_W1, L0_gnn_a_src1, L0_gnn_a_dst1, L0_gnn_b1, L0_gnn_W2, L0_gnn_a_src2, L0_gnn_a_dst2, L0_gnn_b2, L0_gnn_Wu, L0_gnn_bu, L1_gnn_W_fc, L1_gnn_attn_l, L1_gnn_attn_r, L1_gnn_W_res, L2_gnn_W, L2_gnn_b, L3_gnn_W1, L3_gnn_b1, L3_gnn_W2, L3_gnn_b2):
    import jax
    import jax.numpy as jnp

    def _L0_gnn_ref(x, edge_index, norm_g, norm_b, W1, a_src1, a_dst1, b1, W2, a_src2, a_dst2, b2, Wu, bu):
        import jax, jax.numpy as jnp
        import numpy as np
        N = 10000
        E = 2500
        D = 768
        H1, C1 = (4, 192)
        H2, C2 = (2, 96)
        EPS = 1e-05
        NEG_SLOPE = 0.2

        def layer_norm(x, g, b):
            mu = x.mean(-1, keepdims=True)
            var = ((x - mu) ** 2).mean(-1, keepdims=True)
            return (x - mu) * jax.lax.rsqrt(var + EPS) * g + b

        def gat_conv(x, src, dst, W, a_src, a_dst, bias, H, C, n):
            h = (x @ W).reshape(n, H, C)
            s_src = (h * a_src).sum(-1)
            s_dst = (h * a_dst).sum(-1)
            e = jax.nn.leaky_relu(s_src[src] + s_dst[dst], NEG_SLOPE)
            emax = jax.ops.segment_max(e, dst, num_segments=n)
            ee = jnp.exp(e - emax[dst])
            denom = jax.ops.segment_sum(ee, dst, num_segments=n)
            alpha = ee / denom[dst]
            out = jax.ops.segment_sum(alpha[:, :, None] * h[src], dst, num_segments=n)
            return out.reshape(n, H * C) + bias
        loops = jnp.arange(N, dtype=edge_index.dtype)
        src = jnp.concatenate([edge_index[0], loops])
        dst = jnp.concatenate([edge_index[1], loops])
        x_norm = layer_norm(x, norm_g, norm_b)
        out1 = gat_conv(x_norm, src, dst, W1, a_src1, a_dst1, b1, H1, C1, N)
        out2 = gat_conv(out1, src, dst, W2, a_src2, a_dst2, b2, H2, C2, N)
        combined = jnp.concatenate([x, out2], axis=-1)
        return combined @ Wu + bu

    def _L1_gnn_ref(h, W_fc, attn_l, attn_r, W_res, src, dst):
        import jax, jax.numpy as jnp
        import numpy as np
        N = 50000
        E = 250000
        H = 12
        D = 64
        NEG_SLOPE = 0.2
        n = h.shape[0]
        hh = h.reshape(n, H, D)
        ft = jnp.einsum('nhd,ed->nhe', hh, W_fc)
        a1 = jnp.einsum('nhd,hd->nh', ft, attn_l)
        a2 = jnp.einsum('nhd,hd->nh', ft, attn_r)
        e = jax.nn.leaky_relu(a1[src] + a2[dst], negative_slope=NEG_SLOPE)
        m = jax.ops.segment_max(e, dst, num_segments=n)
        ee = jnp.exp(e - m[dst])
        denom = jax.ops.segment_sum(ee, dst, num_segments=n)
        alpha = ee / denom[dst]
        agg = jax.ops.segment_sum(alpha[:, :, None] * ft[src], dst, num_segments=n)
        res = jnp.einsum('nhd,ed->nhe', hh, W_res)
        return jax.nn.relu((res + agg).reshape(n, H * D))

    def _L2_gnn_ref(x, edge_index, W, b):
        import jax, jax.numpy as jnp
        import numpy as np
        N_NODES = 10000
        N_EDGES = 100000
        DIM = 768
        n = x.shape[0]
        loop = jnp.arange(n, dtype=edge_index.dtype)
        src = jnp.concatenate([edge_index[0], loop])
        dst = jnp.concatenate([edge_index[1], loop])
        deg = jax.ops.segment_sum(jnp.ones_like(dst, dtype=x.dtype), dst, num_segments=n)
        deg_inv_sqrt = jnp.where(deg > 0, jax.lax.rsqrt(deg), 0.0)
        norm = deg_inv_sqrt[src] * deg_inv_sqrt[dst]
        h = x @ W
        msg = h[src] * norm[:, None]
        out = jax.ops.segment_sum(msg, dst, num_segments=n)
        return out + b

    def _L3_gnn_ref(x, W1, b1, W2, b2, edge_index):
        import jax, jax.numpy as jnp
        import numpy as np
        N_NODES = 10000
        D = 768
        N_EDGES = 2500

        def gcn_conv(x, W, b, src, dst, n_nodes):
            h = x @ W
            deg = jax.ops.segment_sum(jnp.ones_like(dst, dtype=h.dtype), dst, num_segments=n_nodes)
            dinv = jnp.where(deg > 0, jax.lax.rsqrt(deg), 0.0)
            norm = dinv[src] * dinv[dst]
            msgs = h[src] * norm[:, None]
            out = jax.ops.segment_sum(msgs, dst, num_segments=n_nodes)
            return out + b

        def add_self_loops(edge_index, n_nodes):
            loop = jnp.arange(n_nodes, dtype=edge_index.dtype)
            src = jnp.concatenate([edge_index[0], loop])
            dst = jnp.concatenate([edge_index[1], loop])
            return (src, dst)
        n = x.shape[0]
        src, dst = add_self_loops(edge_index, n)
        h = gcn_conv(x, W1, b1, src, dst, n)
        h = jax.nn.relu(h)
        out = gcn_conv(h, W2, b2, src, dst, n)
        return out
    edge_index = jnp.stack([src, dst])
    x = _layernorm(x + _L0_gnn_ref(x, edge_index, L0_gnn_norm_g, L0_gnn_norm_b, L0_gnn_W1, L0_gnn_a_src1, L0_gnn_a_dst1, L0_gnn_b1, L0_gnn_W2, L0_gnn_a_src2, L0_gnn_a_dst2, L0_gnn_b2, L0_gnn_Wu, L0_gnn_bu), axis=-1)
    x = _layernorm(x + _L1_gnn_ref(x, L1_gnn_W_fc, L1_gnn_attn_l, L1_gnn_attn_r, L1_gnn_W_res, src, dst), axis=-1)
    x = _layernorm(x + _L2_gnn_ref(x, edge_index, L2_gnn_W, L2_gnn_b), axis=-1)
    x = _layernorm(x + _L3_gnn_ref(x, L3_gnn_W1, L3_gnn_b1, L3_gnn_W2, L3_gnn_b2, edge_index), axis=-1)
    return x

_drawn_inputs = setup_inputs


def setup_inputs(seed=0):
    import zlib

    import numpy as np

    out = dict(_drawn_inputs(seed))
    spreads = {'L0_gnn_norm_g': (1.0, 0.2),
     'L0_gnn_norm_b': (0.0, 0.1),
     'L0_gnn_b1': (0.0, 0.1),
     'L0_gnn_b2': (0.0, 0.1),
     'L0_gnn_bu': (0.0, 0.1),
     'L2_gnn_b': (0.0, 0.1),
     'L3_gnn_b1': (0.0, 0.1),
     'L3_gnn_b2': (0.0, 0.1)}
    factors = {'L0_gnn_a_dst1': 7.103, 'L0_gnn_a_src2': 8.0, 'L0_gnn_a_dst2': 8.0}
    for name, (base, spread) in spreads.items():
        noise = np.random.default_rng([zlib.crc32(name.encode()), seed]).standard_normal(out[name].shape)
        drawn = base * np.exp(spread * noise) if base else spread * noise
        out[name] = jnp.asarray(drawn.astype(out[name].dtype))
    for name, factor in factors.items():
        out[name] = (out[name] * factor).astype(out[name].dtype)
    return out
```

```python
import concourse.bass as bass
from concourse import mybir
from concourse.alu_op_type import AluOpType as ALU
from contextlib import ExitStack

F32 = mybir.dt.float32
F32R = mybir.dt.float32r
BF16 = mybir.dt.bfloat16
I32 = mybir.dt.int32
ACT = mybir.ActivationFunctionType
AX = mybir.AxisListType

P = 128
N = 10000
E = 12500
D = 768
NT = (N + P - 1) // P
LAST_ROWS = N - (NT - 1) * P
GROUP = 4
NC = -(-E // (P * GROUP)) * GROUP
NG = NC // GROUP
EP, EC = 125, 100
FAR = 20000
NEG = 1e30
EPS = 1e-5
SLOPE = 0.2
KC = D // P
HALF = D // 2
H_MAX = 12
AGG_W = D + H_MAX
UNROLL = 4
assert EP * EC == E and NT % UNROLL == 3


class Count:

    def __init__(self, sem, per):
        self.sem, self.per = sem, per
        self.base, self.n = 0, 0

    def step(self, t):
        assert self.n in (0, self.per), (self.n, self.per)
        self.base, self.n = t * self.per, 0

    def link(self, eng, ins):
        self.n += 1
        ins.then_inc(self.sem, 1)
        eng.wait_ge(self.sem, self.base + self.n)


def semaphores(nc, ctx, prefix):
    held = []

    def give_back():
        nc.clear_and_free_semaphores(held)
        nc.all_engine_barrier()
    ctx.callback(give_back)

    def sem(name):
        held.append(nc.alloc_semaphore(prefix + name))
        return held[-1]
    return sem


def take_wait(nc, g, scrap):
    c = g["ones"][0:scrap.shape[0], 0:1]
    nc.gpsimd.tensor_tensor(scrap, c, c, ALU.add)


def at_least(t, k):
    return not isinstance(t, int) or t >= k


def over_tiles(eng, step, drain=0):
    for t in range(UNROLL):
        step(t, t, 0)
    with eng.Fori(1, NT // UNROLL) as i:
        for j in range(UNROLL):
            step(i * UNROLL + j, j, i)
    for t in range(NT // UNROLL * UNROLL, NT + drain):
        step(t, t % UNROLL, t // UNROLL)


def back(t, slot, turn, lag):
    return t - lag, (slot - lag) % UNROLL, turn - (1 if slot < lag else 0)


def live(t):
    return not isinstance(t, int) or 0 <= t < NT


def rows_of(t):
    return LAST_ROWS if isinstance(t, int) and t == NT - 1 else P


def tile_rows(ap, t):
    if isinstance(t, int):
        return ap[t * P:t * P + rows_of(t), :]
    return ap[bass.ds(t * P, P), :]


def build(nc, a, out):
    dram = lambda name, shape, dt=F32: nc.dram_tensor(name, shape, dt, kind="Internal").ap()
    packed = dram("packed", ((NC + 2) * P, 2))
    agg = dram("agg", (N, AGG_W))
    agg2 = dram("agg2", (N, 192 + 2))
    h1 = dram("h1", (N, D))
    sc1 = dram("sc1", (N, 10))
    h2 = dram("h2", (N, 192))
    sc2 = dram("sc2", (N, 5))
    x1 = dram("x1", (N, D))
    sc3 = dram("sc3", (N, 25))
    x2 = dram("x2", (N, D))
    x3 = dram("x3", (N, D))
    h3 = dram("h3", (N, D))

    with ExitStack() as ctx:
        def sb(name, shape, dt=F32):
            return ctx.enter_context(nc.sbuf_tensor(name, shape, dt))

        g = {
            "iota": sb("iota", [P, P]), "ident": sb("ident", [P, P]), "upper": sb("upper", [P, P]),
            "ones": sb("ones", [P, P]), "last_lane": sb("last_lane", [P, 1]), "eps": sb("eps", [P, 1]),
            "own": sb("own", [P, NT]), "dinv": sb("dinv", [P, NT]), "own1": sb("own1", [P, NT]),
            "own_d": sb("own_d", [P, NT]), "has_own": sb("has_own", [P, NT]),
            "src_i": sb("src_i", [P, NC], I32), "dst_i": sb("dst_i", [P, NC], I32), "put_i": sb("put_i", [P, NC], I32),
            "seg_end": sb("seg_end", [P, NC]), "carry_end": sb("carry_end", [P, NC]),
            "node": sb("node", [P, 2 * NT]),
            "total_i": sb("total_i", [P, 1], I32), "edge_dinv": sb("edge_dinv", [P, NC]),
            "same_f": sb("same_f", [NC, H_MAX * P]), "same_b": sb("same_b", [NC, H_MAX * P]),
            "pen_f": sb("pen_f", [NC, H_MAX * P]), "pen_b": sb("pen_b", [NC, H_MAX * P]),
            "cont_f": sb("cont_f", [NC, P]), "cont_b": sb("cont_b", [NC, P]),
            "row_f": sb("row_f", [H_MAX, NC]), "row_b": sb("row_b", [H_MAX, NC]),
            "alpha": sb("alpha", [P, NC, H_MAX]), "own_w": sb("own_w", [P, NC, H_MAX]),
        }
        prepare(nc, g, a, packed, agg, agg2)
        dense_pass(nc, g, "proj", "project", a, h1, sc1, row=a["x"], weights=a["L0_gnn_W1"], bias=a["L0_gnn_norm_b"])
        attention(nc, g, "l0a", 4, sc1, 10, 8, 9)
        gather_sum(nc, g, "l0a", h1, D, 4, agg)
        dense_pass(nc, g, "att", "attend", a, h2, sc2, row=h1, agg=agg, weights=a["L0_gnn_W2"], bias=a["L0_gnn_b1"])
        attention(nc, g, "l0b", 2, sc2, 5, 4, None)
        gather_sum(nc, g, "l0b", h2, 192, 2, agg2)
        dense_pass(nc, g, "upd", "update", a, x1, sc3, row=h2, agg=agg2, res=a["x"], weights=a["L0_gnn_Wu"], bias=a["L0_gnn_b2"])
        attention(nc, g, "l1", 12, sc3, 25, 24, None)
        gather_sum(nc, g, "l1", x1, D, 12, agg)
        dense_pass(nc, g, "hds", "heads", a, x2, row=x1, agg=agg)
        gather_sum(nc, g, "l2", x2, D, 0, agg)
        dense_pass(nc, g, "cv2", "conv", a, x3, row=x2, agg=agg, res=x2, weights=a["L2_gnn_W"], bias=a["L2_gnn_b"])
        gather_sum(nc, g, "l3a", x3, D, 0, agg)
        dense_pass(nc, g, "c3a", "conv", a, h3, row=x3, agg=agg, weights=a["L3_gnn_W1"], bias=a["L3_gnn_b1"])
        gather_sum(nc, g, "l3b", h3, D, 0, agg)
        dense_pass(nc, g, "c3b", "conv", a, out, row=h3, agg=agg, res=x3, weights=a["L3_gnn_W2"], bias=a["L3_gnn_b2"])


def prepare(nc, g, a, packed, agg, agg2):
    with ExitStack() as ctx:
        def sb(name, shape, dt=F32):
            return ctx.enter_context(nc.sbuf_tensor("pr_" + name, shape, dt))

        sem = semaphores(nc, ctx, "pr_")

        s_i, d_i = sb("s_i", [EP, EC], I32), sb("d_i", [EP, EC], I32)
        hi_i, lo_i = sb("hi_i", [EP, EC], I32), sb("lo_i", [EP, EC], I32)
        hi_f, lo_f = sb("hi_f", [EP, EC]), sb("lo_f", [EP, EC])
        rec = sb("rec", [EP, EC, 2])
        diff, same = sb("diff", [EP, EC]), sb("same", [EP, EC])
        rank, zero = sb("rank", [EP, EC]), sb("zero", [EP, EC])
        rank_i = sb("rank_i", [EP, EC], I32)
        before = sb("before", [P, P])
        scrap = sb("scrap", [P, 1])
        ix4, rec4 = sb("ix4", [EP, GROUP], I32), sb("rec4", [EP, GROUP, 2])
        lo_hot = sb("lo_hot", [EP, EC * P], BF16)
        hi_hot = sb("hi_hot", [EP, EC * 2 * NT], BF16)
        lo_hot3 = lo_hot[:, :].rearrange("p (c j) -> p c j", c=EC)
        hi_hot4 = hi_hot[:, :].rearrange("p (c k t) -> p c k t", c=EC, k=2)
        pad = sb("pad", [P, (NC + 2) * 2])
        zrow = sb("zrow", [P, AGG_W])
        sd_c = sb("sd_c", [P, NC, 2])
        sd_r = sb("sd_r", [NC, P, 2])
        prv, nxt = sb("prv", [NC, 1]), sb("nxt", [NC, 1])
        is_last, end_r = sb("is_last", [NC, P]), sb("end_r", [NC, P])
        val, carry_r = sb("val", [NC, P]), sb("carry_r", [NC, 1])
        last_c, tmp_c = sb("last_c", [P, NC]), sb("tmp_c", [P, NC])
        deg, sq = sb("deg", [P, NT]), sb("sq", [P, NT])
        all_f, all_b = sb("all_f", [NC, 1]), sb("all_b", [NC, 1])
        ps = ctx.enter_context(nc.psum_tensor("pr_ps", [P, 2 * NT], F32))
        ps2 = ctx.enter_context(nc.psum_tensor("pr_ps2", [P, 512], F32))
        ps3 = ctx.enter_context(nc.psum_tensor("pr_ps3", [P, 512], F32))

        loaded, consts, hots, hist = sem("loaded"), sem("consts"), sem("hots"), sem("hist")
        dve_self, pads, packs, zeros = sem("dve_self"), sem("pads"), sem("packs"), sem("zeros")
        slots = sem("slots")
        ranks, padded, counted, offset = sem("ranks"), sem("padded"), sem("counted"), sem("offset")
        reloaded, rooted, rows_done, turned = sem("reloaded"), sem("rooted"), sem("rows_done"), sem("turned")
        block = ctx.enter_context(nc.Block())

        @block.sync
        def _(sp):
            sp.dma_start(s_i[:, :], a["src"].rearrange("(p c) -> p c", p=EP)).then_inc(loaded, 16)
            sp.dma_start(d_i[:, :], a["dst"].rearrange("(p c) -> p c", p=EP)).then_inc(loaded, 16)
            sp.wait_ge(pads, 1)
            sp.dma_start(packed.rearrange("(p c) w -> p (c w)", p=P), pad[:, :]).then_inc(padded, 16)
            sp.wait_ge(pads, 2)

            def clear(t, slot, turn):
                sp.dma_start(tile_rows(agg, t), zrow[0:rows_of(t), :]).then_inc(zeros, 16)
                sp.dma_start(tile_rows(agg2, t), zrow[0:rows_of(t), 0:194]).then_inc(zeros, 16)
            over_tiles(sp, clear)
            sp.wait_ge(packs, 16 * EC)
            sp.dma_start(sd_c[:, :, :], packed[P:P + NC * P, :].rearrange("(c p) w -> p c w", p=P)).then_inc(reloaded, 16)
            sp.dma_start(sd_r[:, :, :], packed[P:P + NC * P, :].rearrange("(c j) w -> c j w", j=P)).then_inc(reloaded, 16)
            sp.dma_start(prv[:, :], packed.rearrange("(c j) w -> c j w", j=P)[0:NC, P - 1, 1:2],
                         allow_slow_non_contiguous=True).then_inc(reloaded, 16)
            sp.dma_start(nxt[:, :], packed.rearrange("(c j) w -> c j w", j=P)[2:NC + 2, 0, 1:2],
                         allow_slow_non_contiguous=True).then_inc(reloaded, 16)
            sp.wait_ge(zeros, 32 * NT)

        @block.gpsimd
        def _(pool):
            nc.gpsimd.memset(pad[:, :], float(FAR)).then_inc(pads, 1)
            nc.gpsimd.memset(zrow[:, :], 0.0).then_inc(pads, 1)
            nc.gpsimd.iota(g["iota"][:, :], [[1, P]], base=0, channel_multiplier=0,
                           allow_small_or_imprecise_dtypes=True).then_inc(consts, 1)
            nc.gpsimd.memset(g["ones"][:, :], 1.0).then_inc(consts, 1)
            nc.gpsimd.memset(g["ident"][:, :], 0.0).then_inc(consts, 1)
            nc.gpsimd.memset(g["eps"][:, :], EPS).then_inc(consts, 1)
            nc.gpsimd.memset(g["last_lane"][:, :], 0.0).then_inc(consts, 1)
            nc.gpsimd.memset(g["alpha"][:, :, :], 0.0).then_inc(consts, 1)
            nc.gpsimd.memset(g["own_w"][:, :, :], 0.0).then_inc(consts, 1)
            pool.wait_ge(consts, 7)
            nc.gpsimd.affine_select(out=g["ident"][:, :], in_=g["ident"][:, :], compare_op=ALU.not_equal, fill=1.0,
                                    base=0, pattern=[[-1, P]], channel_multiplier=1).then_inc(consts, 1)
            nc.gpsimd.affine_select(out=g["upper"][:, :], in_=g["ones"][:, :], compare_op=ALU.is_ge, fill=0.0,
                                    base=0, pattern=[[1, P]], channel_multiplier=-1).then_inc(consts, 1)
            nc.gpsimd.affine_select(out=before[:, :], in_=g["ones"][:, :], compare_op=ALU.is_ge, fill=0.0,
                                    base=-1, pattern=[[1, P]], channel_multiplier=-1).then_inc(consts, 1)
            nc.gpsimd.affine_select(out=g["last_lane"][:, :], in_=g["last_lane"][:, :], compare_op=ALU.not_equal,
                                    fill=1.0, base=-(P - 1), pattern=[[0, 1]], channel_multiplier=1).then_inc(consts, 1)
            pool.wait_ge(padded, 16)
            pool.wait_ge(ranks, 1)

            bound = pool.to_reg((NC + 2) * P - 1)

            def place(first, turn):
                if first:
                    pool.wait_ge(packs, turn * (16 * GROUP))
                nc.gpsimd.tensor_copy(ix4[:, :], rank_i[:, bass.ds(turn * GROUP, GROUP)]).then_inc(slots, 1)
                nc.gpsimd.tensor_copy(rec4[:, :, :], rec[:, bass.ds(turn * GROUP, GROUP), :]).then_inc(slots, 1)
                pool.wait_ge(slots, turn * 2 + 2)
                take_wait(nc, g, scrap[:, 0:1])
                for j in range(GROUP):
                    nc.gpsimd.indirect_dma_start(packed, bass.IndirectOffsetOnAxis(ap=ix4[:, j:j + 1], axis=0),
                                                 rec4[:, j, :], None, bounds_check=bound,
                                                 oob_is_err=False).then_inc(packs, 16)
            place(False, 0)
            with pool.Fori(1, EC // GROUP) as i:
                place(True, i)
            pool.wait_ge(packs, 16 * EC)

        @block.vector
        def _(dve):
            v, n = nc.vector, [0]

            def link(ins):
                n[0] += 1
                ins.then_inc(dve_self, 1)
                dve.wait_ge(dve_self, n[0])

            dve.wait_ge(consts, 11)
            dve.wait_ge(loaded, 32)
            link(v.memset(zero[:, :], 0.0))
            link(v.tensor_copy(rec[:, :, 0], s_i[:, :]))
            link(v.tensor_copy(rec[:, :, 1], d_i[:, :]))
            link(v.tensor_tensor(diff[:, :], rec[:, :, 0], rec[:, :, 1], ALU.not_equal))
            link(v.tensor_tensor(same[:, :], rec[:, :, 0], rec[:, :, 1], ALU.is_equal))
            v.tensor_tensor_scan(rank[:, :], diff[:, :], zero[:, :], 0.0, ALU.add, ALU.add).then_inc(counted, 1)
            link(v.tensor_scalar(hi_i[:, :], d_i[:, :], 7, None, ALU.arith_shift_right))
            link(v.tensor_scalar(lo_i[:, :], d_i[:, :], P - 1, None, ALU.bitwise_and))
            link(v.tensor_copy(hi_f[:, :], hi_i[:, :]))
            link(v.tensor_copy(lo_f[:, :], lo_i[:, :]))
            dve.wait_ge(offset, 1)
            link(v.tensor_scalar(rank[:, :], rank[:, :], ps2[0:EP, 0:1], float(P - 1 - FAR), ALU.add, ALU.add))
            link(v.tensor_tensor(rank[:, :], rank[:, :], diff[:, :], ALU.mult))
            link(v.tensor_scalar(rank[:, :], rank[:, :], float(FAR), None, ALU.add))
            v.tensor_copy(rank_i[:, :], rank[:, :]).then_inc(ranks, 1)
            link(v.tensor_copy(g["total_i"][:, :], ps2[:, 1:2]))
            lo_b = lo_f[:, :].unsqueeze(2).to_broadcast([EP, EC, P])
            hi_b = hi_f[:, :].unsqueeze(2).to_broadcast([EP, EC, NT])
            same_b = same[:, :].unsqueeze(2).to_broadcast([EP, EC, NT])
            iota_p = g["iota"][0:EP, :].unsqueeze(1).to_broadcast([EP, EC, P])
            iota_t = g["iota"][0:EP, 0:NT].unsqueeze(1).to_broadcast([EP, EC, NT])
            link(v.tensor_tensor(lo_hot3, lo_b, iota_p, ALU.is_equal))
            link(v.tensor_tensor(hi_hot4[:, :, 0, :], hi_b, iota_t, ALU.is_equal))
            v.tensor_tensor(hi_hot4[:, :, 1, :], hi_hot4[:, :, 0, :], same_b, ALU.mult).then_inc(hots, 1)
            dve.wait_ge(hist, 1)
            link(v.tensor_scalar(deg[:, :], ps[:, 0:NT], 1.0, None, ALU.add))
            link(v.tensor_copy(g["own"][:, :], ps[:, NT:2 * NT]))
            v.tensor_scalar(g["own1"][:, :], g["own"][:, :], 1.0, None, ALU.add).then_inc(rows_done, 1)
            link(v.tensor_scalar(g["has_own"][:, :], g["own"][:, :], 1.0, None, ALU.min))
            dve.wait_ge(rooted, 1)
            link(v.reciprocal(g["dinv"][:, :], sq[:, :]))
            link(v.tensor_tensor(g["own_d"][:, :], g["own1"][:, :], g["dinv"][:, :], ALU.mult))
            node = g["node"][:, :].rearrange("p (t k) -> p t k", k=2)
            link(v.tensor_copy(node[:, :, 0], g["own1"][:, :]))
            link(v.tensor_copy(node[:, :, 1], g["dinv"][:, :]))
            dve.wait_ge(reloaded, 64)
            dst = sd_r[:, :, 1]
            H = H_MAX
            f3 = g["same_f"][:, :].rearrange("c (h j) -> c h j", h=H)
            b3 = g["same_b"][:, :].rearrange("c (h j) -> c h j", h=H)
            link(v.memset(f3, 0.0))
            link(v.memset(b3, 0.0))
            link(v.tensor_tensor(f3[:, 0, 1:P], sd_r[:, 1:P, 1], sd_r[:, 0:P - 1, 1], ALU.is_equal))
            link(v.tensor_copy(b3[:, 0, 0:P - 1], f3[:, 0, 1:P]))
            link(v.tensor_copy(f3[:, 1:H, :], f3[:, 0, :].unsqueeze(1).to_broadcast([NC, H - 1, P])))
            link(v.tensor_copy(b3[:, 1:H, :], b3[:, 0, :].unsqueeze(1).to_broadcast([NC, H - 1, P])))
            link(v.tensor_scalar(g["pen_f"][:, :], g["same_f"][:, :], -1.0, NEG, ALU.add, ALU.mult))
            link(v.tensor_scalar(g["pen_b"][:, :], g["same_b"][:, :], -1.0, NEG, ALU.add, ALU.mult))
            link(v.tensor_tensor(g["cont_f"][:, :], dst, prv[:, :].to_broadcast([NC, P]), ALU.is_equal))
            link(v.tensor_tensor(g["cont_b"][:, :], dst, nxt[:, :].to_broadcast([NC, P]), ALU.is_equal))
            link(v.tensor_copy(all_f[:, :], g["cont_f"][:, P - 1:P]))
            v.tensor_copy(all_b[:, :], g["cont_b"][:, 0:1]).then_inc(rows_done, 1)
            link(v.tensor_copy(is_last[:, 0:P - 1], b3[:, 0, 0:P - 1]))
            link(v.tensor_copy(is_last[:, P - 1:P], g["cont_b"][:, P - 1:P]))
            link(v.tensor_scalar(is_last[:, :], is_last[:, :], -1.0, 1.0, ALU.mult, ALU.add))
            link(v.tensor_scalar(val[:, :], b3[:, 0, :], float(FAR), None, ALU.mult))
            link(v.tensor_tensor(val[:, :], val[:, :], g["iota"][0:NC, :], ALU.add))
            link(v.tensor_tensor_scan(end_r[:, ::-1], val[:, ::-1], val[:, ::-1], float(FAR), ALU.min, ALU.min))
            link(v.tensor_scalar(carry_r[:, :], end_r[:, 0:1], 1.0, None, ALU.add))
            link(v.tensor_tensor(carry_r[:, :], carry_r[:, :], g["cont_f"][:, 0:1], ALU.mult))
            v.tensor_scalar(carry_r[:, :], carry_r[:, :], -1.0, None, ALU.add).then_inc(rows_done, 1)
            dve.wait_ge(turned, 1)
            link(v.tensor_copy(g["row_f"][:, :], ps3[0:H, 0:NC]))
            link(v.tensor_copy(g["row_b"][:, :], ps3[0:H, 128:128 + NC]))
            link(v.tensor_copy(g["carry_end"][:, :], ps3[:, 256:256 + NC]))
            link(v.tensor_copy(g["seg_end"][:, :], ps2[:, 128:128 + NC]))
            link(v.tensor_copy(last_c[:, :], ps2[:, 256:256 + NC]))
            link(v.tensor_copy(g["src_i"][:, :], sd_c[:, :, 0]))
            link(v.tensor_copy(g["dst_i"][:, :], sd_c[:, :, 1]))
            link(v.tensor_scalar(tmp_c[:, :], sd_c[:, :, 1], -float(FAR), None, ALU.add))
            link(v.tensor_tensor(tmp_c[:, :], tmp_c[:, :], last_c[:, :], ALU.mult))
            link(v.tensor_scalar(tmp_c[:, :], tmp_c[:, :], float(FAR), None, ALU.add))
            link(v.tensor_copy(g["put_i"][:, :], tmp_c[:, :]))

        @block.scalar
        def _(act):
            act.wait_ge(rows_done, 1)
            nc.scalar.activation(sq[:, :], deg[:, :], ACT.Sqrt).then_inc(rooted, 1)

        @block.tensor
        def _(pe):
            pe.wait_ge(consts, 11)
            pe.wait_ge(counted, 1)
            nc.tensor.matmul(ps2[0:EP, 0:1], before[0:EP, 0:EP], rank[:, EC - 1:EC], start=True, stop=True)
            nc.tensor.matmul(ps2[:, 1:2], g["ones"][0:EP, :], rank[:, EC - 1:EC], start=True, stop=True).then_inc(offset, 1)
            pe.wait_ge(hots, 1)

            def count(c, start, stop):
                return nc.tensor.matmul(ps[:, :], lo_hot[:, bass.ds(c * P, P)], hi_hot[:, bass.ds(c * 2 * NT, 2 * NT)],
                                        start=start, stop=stop, skip_group_check=True)
            count(0, True, False)
            with pe.Fori(1, EC - 1) as c:
                count(c, False, False)
            count(EC - 1, False, True).then_inc(hist, 1)
            pe.wait_ge(rows_done, 3)
            ident = g["ident"][0:NC, 0:NC]
            nc.tensor.matmul(ps3[0:H_MAX, 0:NC], all_f[:, :].to_broadcast([NC, H_MAX]), ident, start=True, stop=True)
            nc.tensor.matmul(ps3[0:H_MAX, 128:128 + NC], all_b[:, :].to_broadcast([NC, H_MAX]), ident, start=True, stop=True)
            nc.tensor.matmul(ps3[:, 256:256 + NC], carry_r[:, :].to_broadcast([NC, P]), ident, start=True, stop=True)
            nc.tensor.transpose(ps2[:, 128:128 + NC], end_r[:, :], ident)
            nc.tensor.transpose(ps2[:, 256:256 + NC], is_last[:, :], ident).then_inc(turned, 1)


def attention(nc, g, tag, H, scores, W, own_col, dinv_col):
    with ExitStack() as ctx:
        def sb(name, shape, dt=F32):
            return ctx.enter_context(nc.sbuf_tensor(f"{tag}_{name}", shape, dt))

        sem = semaphores(nc, ctx, f"{tag}_")

        from_src, from_dst = sb("from_src", [P, NC, W]), sb("from_dst", [P, NC, W])
        z, zo = sb("z", [P, H, NC]), sb("zo", [P, H, NC])
        got = sb("got", [P, 2, GROUP, W])
        scrap = sb("scrap", [P, 1])
        ix = sb("ix", [P, 2, GROUP], I32)
        z_edge = sb("z_edge", [H, NC])
        cpen = sb("cpen", [NC, P])
        own_c = sb("own_c", [P, NC])
        t0, t1 = sb("t0", [P, H, NC]), sb("t1", [P, H, NC])
        R = lambda name: sb(name, [NC, H * P])
        zr, zor, fwd, bwd, top, w, wo, w_tmp = R("zr"), R("zor"), R("fwd"), R("bwd"), R("top"), R("w"), R("wo"), R("w_tmp")
        own_r = sb("own_r", [NC, P])
        edge, edge_t = sb("edge", [NC, H]), sb("edge_t", [H, NC + 2])
        rows = sb("rows", [H, NC])
        psz = ctx.enter_context(nc.psum_tensor(f"{tag}_psz", [P, 2048], F32))
        pst = ctx.enter_context(nc.psum_tensor(f"{tag}_pst", [P, 512], F32))
        psb = ctx.enter_context(nc.psum_tensor(f"{tag}_psb", [P, 512], F32))
        zeroed, gathered, scored, turned = sem("zeroed"), sem("gathered"), sem("scored"), sem("turned")
        dve_self, edges, edges_up, carries, carries_up = (sem("dve_self"), sem("edges"), sem("edges_up"),
                                                          sem("carries"), sem("carries_up"))
        indexed, copied, taken = sem("indexed"), sem("copied"), sem("taken")
        shifted, expd, back, freed = sem("shifted"), sem("expd"), sem("back"), sem("freed")
        block = ctx.enter_context(nc.Block())
        HW = H * P
        per_bank = 4

        @block.gpsimd
        def _(pool):
            nc.gpsimd.memset(from_src[:, :, :], 0.0).then_inc(zeroed, 1)
            nc.gpsimd.memset(from_dst[:, :, :], 0.0).then_inc(zeroed, 1)
            nc.gpsimd.memset(got[:, :, :, :], 0.0).then_inc(zeroed, 1)
            nc.gpsimd.memset(ix[:, :, :], 0).then_inc(zeroed, 1)
            pool.wait_ge(zeroed, 4)

            def fetch(first, turn):
                if not first:
                    pool.wait_ge(copied, turn)
                nc.gpsimd.tensor_copy(ix[:, 0, :], g["src_i"][:, bass.ds(turn * GROUP, GROUP)]).then_inc(indexed, 1)
                nc.gpsimd.tensor_copy(ix[:, 1, :], g["dst_i"][:, bass.ds(turn * GROUP, GROUP)]).then_inc(indexed, 1)
                for k in range(2):
                    for j in range(GROUP):
                        if k == 0 and j == 0:
                            pool.wait_ge(indexed, turn * 2 + 2)
                            take_wait(nc, g, scrap[:, 0:1])
                        nc.gpsimd.indirect_dma_start(got[:, k, j, :], None, scores,
                                                     bass.IndirectOffsetOnAxis(ap=ix[:, k, j:j + 1], axis=0),
                                                     bounds_check=N - 1, oob_is_err=False).then_inc(gathered, 16)
            fetch(True, 0)
            total = pool.value_load(g["total_i"][0:1, 0:1], min_val=0, max_val=E)
            with pool.Fori(1, NG) as i:
                with pool.If(total > i * (GROUP * P)):
                    fetch(False, i)

        @block.vector
        def _(dve):
            v, n = nc.vector, [0]

            def link(ins):
                n[0] += 1
                ins.then_inc(dve_self, 1)
                dve.wait_ge(dve_self, n[0])

            def take(turn):
                dve.wait_ge(gathered, turn * (32 * GROUP) + 32 * GROUP)
                v.tensor_copy(from_src[:, bass.ds(turn * GROUP, GROUP), :], got[:, 0, :, :]).then_inc(taken, 1)
                v.tensor_copy(from_dst[:, bass.ds(turn * GROUP, GROUP), :], got[:, 1, :, :]).then_inc(taken, 1)
                dve.wait_ge(taken, turn * 2 + 2)
                dve.sem_inc(copied, 1)
            dve.wait_ge(zeroed, 4)
            take(0)
            total = dve.value_load(g["total_i"][0:1, 0:1], min_val=0, max_val=E)
            with dve.Fori(1, NG) as i:
                with dve.If(total > i * (GROUP * P)):
                    take(i)
            ssrc = from_src[:, :, 0:H].rearrange("p c h -> p h c")
            sdst = from_dst[:, :, H:2 * H].rearrange("p c h -> p h c")
            osrc = from_dst[:, :, 0:H].rearrange("p c h -> p h c")
            if dinv_col is not None:
                link(v.tensor_copy(g["edge_dinv"][:, :], from_src[:, :, dinv_col]))
            link(v.tensor_copy(own_c[:, :], from_dst[:, :, own_col]))
            for x, y, dst in ((ssrc, sdst, z), (osrc, sdst, zo)):
                link(v.tensor_tensor(t0[:, :, :], x, y, ALU.add))
                link(v.scalar_tensor_tensor(dst[:, :, :], t0[:, :, :], SLOPE, t0[:, :, :], ALU.mult, ALU.max))
            link(v.tensor_scalar(t1[:, 0, :], own_c[:, :], 1.0, -1.0, ALU.min, ALU.add))
            link(v.tensor_scalar(t1[:, 0, :], t1[:, 0, :], NEG, None, ALU.mult))
            v.tensor_tensor(zo[:, :, :], zo[:, :, :], t1[:, 0:1, :].to_broadcast([P, H, NC]), ALU.add).then_inc(scored, 1)
            dve.wait_ge(turned, 1)
            link(v.tensor_copy(own_r[:, :], psb[0:NC, 0:P]))
            v.tensor_copy(zr[:, :], psz[0:NC, 0:HW]).then_inc(freed, 1)
            dve.wait_ge(turned, 2)
            link(v.tensor_copy(zor[:, :], psz[0:NC, 0:HW]))

            k = [0]

            def total_of(vals, into, forward, is_max):
                same = g[("pen_" if is_max else "same_") + ("f" if forward else "b")][:, 0:HW]
                cont = g["cont_f" if forward else "cont_b"]
                whole = g["row_f" if forward else "row_b"][0:H, :]
                none, op = (-NEG, ALU.max) if is_max else (0.0, ALU.add)
                hold = ALU.add if is_max else ALU.mult
                turn = (lambda x: x) if forward else (lambda x: x[:, ::-1])
                link(v.tensor_tensor_scan(turn(into[:, :]), turn(same), turn(vals[:, :]), none, hold, op))
                col = into[:, :].rearrange("c (h j) -> c h j", h=H)[:, :, P - 1 if forward else 0]
                v.tensor_copy(edge[:, :], col).then_inc(edges, 1)
                k[0] += 1
                dve.wait_ge(edges_up, k[0])
                src = pst[0:H, 0:NC]
                link(v.memset(edge_t[:, :], none))
                if is_max:
                    link(v.tensor_scalar(rows[:, :], whole, -1.0, NEG, ALU.add, ALU.mult))
                else:
                    link(v.tensor_copy(rows[:, :], whole))
                link(v.tensor_copy(z_edge[0:H, :], src))
                link(v.tensor_tensor_scan(turn(edge_t[:, 1:NC + 1]), turn(rows[:, :]), turn(z_edge[0:H, :]), none, hold, op))
                v.tensor_copy(z_edge[0:H, :], edge_t[:, 0:NC] if forward else edge_t[:, 2:NC + 2]).then_inc(carries, 1)
                dve.wait_ge(carries_up, k[0])
                i3 = into[:, :].rearrange("c (h j) -> c h j", h=H)
                x3 = w_tmp[:, :].rearrange("c (h j) -> c h j", h=H)
                cb = cont[:, :].unsqueeze(1).to_broadcast([NC, H, P])
                hand = pst[0:NC, 128:128 + H].unsqueeze(2).to_broadcast([NC, H, P])
                if is_max:
                    link(v.tensor_scalar(cpen[:, :], cont[:, :], -1.0, NEG, ALU.add, ALU.mult))
                    link(v.tensor_tensor(x3, hand, cpen[:, :].unsqueeze(1).to_broadcast([NC, H, P]), ALU.add))
                else:
                    link(v.tensor_tensor(x3, hand, cb, ALU.mult))
                link(v.tensor_tensor(into[:, :], into[:, :], w_tmp[:, :], op))

            total_of(zr, fwd, True, True)
            total_of(zr, bwd, False, True)
            link(v.tensor_tensor(top[:, :], fwd[:, :], bwd[:, :], ALU.max))
            link(v.tensor_tensor(top[:, :], top[:, :], zor[:, :], ALU.max))
            link(v.tensor_tensor(zr[:, :], zr[:, :], top[:, :], ALU.subtract))
            v.tensor_tensor(zor[:, :], zor[:, :], top[:, :], ALU.subtract).then_inc(shifted, 1)
            dve.wait_ge(expd, 2)
            wo3 = wo[:, :].rearrange("c (h j) -> c h j", h=H)
            ob = own_r[:, :].unsqueeze(1).to_broadcast([NC, H, P])
            link(v.tensor_tensor(wo3, wo3, ob, ALU.mult))
            total_of(w, fwd, True, False)
            total_of(w, bwd, False, False)
            link(v.tensor_tensor(top[:, :], fwd[:, :], bwd[:, :], ALU.add))
            link(v.tensor_tensor(top[:, :], top[:, :], w[:, :], ALU.subtract))
            link(v.tensor_tensor(top[:, :], top[:, :], wo[:, :], ALU.add))
            link(v.reciprocal(fwd[:, :], top[:, :]))
            link(v.tensor_tensor(w[:, :], w[:, :], fwd[:, :], ALU.mult))
            v.tensor_tensor(wo[:, :], wo[:, :], fwd[:, :], ALU.mult).then_inc(back, 1)
            for m, dst in ((1, "alpha"), (2, "own_w")):
                dve.wait_ge(turned, 2 + m)
                ph = psz[:, 0:HW].rearrange("p (h c) -> p c h", h=H)[:, 0:NC, :]
                if m == 1:
                    v.tensor_copy(g[dst][:, :, 0:H], ph).then_inc(freed, 1)
                else:
                    link(v.tensor_scalar(t1[:, 0, :], own_c[:, :], 1.0, None, ALU.min))
                    link(v.tensor_tensor(g[dst][:, :, 0:H], ph,
                                         t1[:, 0, :].unsqueeze(2).to_broadcast([P, NC, H]), ALU.subtract))

        @block.scalar
        def _(act):
            act.wait_ge(shifted, 1)
            nc.scalar.activation(w[:, :], zr[:, :], ACT.Exp).then_inc(expd, 1)
            nc.scalar.activation(wo[:, :], zor[:, :], ACT.Exp).then_inc(expd, 1)

        @block.tensor
        def _(pe):
            pe.wait_ge(scored, 1)
            for h in range(H):
                nc.tensor.transpose(psz[0:NC, h * P:(h + 1) * P], z[:, h, :], g["ident"][:, :])
            nc.tensor.transpose(psb[0:NC, 0:P], own_c[:, :], g["ident"][:, :]).then_inc(turned, 1)
            pe.wait_ge(freed, 1)
            for h in range(H):
                last = nc.tensor.transpose(psz[0:NC, h * P:(h + 1) * P], zo[:, h, :], g["ident"][:, :])
            last.then_inc(turned, 1)
            for k in range(1, 5):
                pe.wait_ge(edges, k)
                nc.tensor.transpose(pst[0:H, 0:NC], edge[:, :], g["ident"][0:NC, 0:NC]).then_inc(edges_up, 1)
                pe.wait_ge(carries, k)
                nc.tensor.transpose(pst[0:NC, 128:128 + H], z_edge[0:H, :], g["ident"][0:H, 0:H]).then_inc(carries_up, 1)
            pe.wait_ge(back, 1)
            for m, x in ((1, w), (2, wo)):
                if m == 2:
                    pe.wait_ge(freed, 2)
                for h in range(H):
                    last = nc.tensor.transpose(psz[:, h * P:h * P + NC], x[:, h * P:(h + 1) * P], g["ident"][0:NC, 0:NC])
                last.then_inc(turned, 1)


def gather_sum(nc, g, tag, table, F, H, agg):
    with ExitStack() as ctx:
        def sb(name, shape, dt=F32):
            return ctx.enter_context(nc.sbuf_tensor(f"{tag}s_{name}", shape, dt))

        sem = semaphores(nc, ctx, f"{tag}s_")

        rows = sb("rows", [P, GROUP, D])
        scrap = sb("scrap", [P, 1 + GROUP])
        sel, car = sb("sel", [P, 2, P]), sb("car", [P, 2, P])
        sums = sb("sums", [P, GROUP, AGG_W])
        ix = sb("ix", [P, 2, GROUP], I32)
        ps = [ctx.enter_context(nc.psum_tensor(f"{tag}s_ps{i}", [P, 2, 512], F32)) for i in range(2)]
        cleared, indexed, ready, summed, kept = sem("cleared"), sem("indexed"), sem("ready"), sem("summed"), sem("kept")
        arrived = [sem(f"arrived{j}") for j in range(GROUP)]
        stored = [sem(f"stored{j}") for j in range(GROUP)]
        block = ctx.enter_context(nc.Block())
        step = F // 2
        KEPT = 2 if H else 1

        def groups(eng, body, skipped=None):
            body(0, True)
            total = eng.value_load(g["total_i"][0:1, 0:1], min_val=0, max_val=E)
            with eng.Fori(1, NG) as i:
                with eng.If(total > i * (GROUP * P)):
                    body(i, False)

        @block.gpsimd
        def _(pool):
            nc.gpsimd.memset(rows[:, :, :], 0.0).then_inc(cleared, 1)
            nc.gpsimd.memset(sums[:, :, :], 0.0).then_inc(cleared, 1)
            nc.gpsimd.memset(ix[:, :, :], 0).then_inc(cleared, 1)
            pool.wait_ge(cleared, 3)

            def put(turn, j):
                pool.wait_ge(kept, (turn * GROUP + (j + 1)) * KEPT)
                take_wait(nc, g, scrap[:, j + 1:j + 2])
                nc.gpsimd.indirect_dma_start(agg, bass.IndirectOffsetOnAxis(ap=ix[:, 1, j:j + 1], axis=0),
                                             sums[:, j, 0:agg.shape[1]], None,
                                             bounds_check=N - 1, oob_is_err=False).then_inc(stored[j], 16)

            def body(turn, first):
                if not first:
                    for j in range(GROUP):
                        pool.wait_ge(stored[j], turn * 16)
                nc.gpsimd.tensor_copy(ix[:, 0, :], g["src_i"][:, bass.ds(turn * GROUP, GROUP)]).then_inc(indexed, 1)
                nc.gpsimd.tensor_copy(ix[:, 1, :], g["put_i"][:, bass.ds(turn * GROUP, GROUP)]).then_inc(indexed, 1)
                pool.wait_ge(indexed, turn * 2 + 2)
                take_wait(nc, g, scrap[:, 0:1])
                for j in range(GROUP):
                    nc.gpsimd.indirect_dma_start(rows[:, j, 0:F], None, table,
                                                 bass.IndirectOffsetOnAxis(ap=ix[:, 0, j:j + 1], axis=0),
                                                 bounds_check=N - 1, oob_is_err=False).then_inc(arrived[j], 16)
                for j in range(GROUP):
                    put(turn, j)
                    pool.wait_ge(stored[j], turn * 16 + 16)
            groups(pool, body)

        @block.vector
        def _(dve):
            v = nc.vector
            dve.wait_ge(cleared, 3)

            def body(turn, first):
                for j in range(GROUP):
                    c = turn * GROUP + j
                    if not first or j >= 2:
                        dve.wait_ge(summed, c - 1)
                    v.scalar_tensor_tensor(sel[:, j % 2, :], g["iota"][:, :], g["seg_end"][:, bass.ds(c, 1)],
                                           g["upper"][:, :], ALU.is_le, ALU.mult).then_inc(ready, 1)
                    v.tensor_scalar(car[:, j % 2, :], g["iota"][:, :], g["carry_end"][:, bass.ds(c, 1)],
                                    g["last_lane"][:, :], ALU.is_le, ALU.mult).then_inc(ready, 1)
                    dve.wait_ge(arrived[j], turn * 16 + 16)
                    if H:
                        r3 = rows[:, j, 0:F].rearrange("p (h f) -> p h f", h=H)
                        al = g["alpha"][:, bass.ds(c, 1), 0:H].rearrange("p c h -> p (c h)")
                        v.tensor_tensor(r3, r3, al.unsqueeze(2).to_broadcast([P, H, F // H]), ALU.mult).then_inc(ready, 1)
                    else:
                        dve.wait_ge(ready, c * 3 + 2)
                        v.tensor_scalar(sel[:, j % 2, :], sel[:, j % 2, :], g["edge_dinv"][:, bass.ds(c, 1)], None,
                                        ALU.mult).then_inc(ready, 1)
            groups(dve, body)

        @block.tensor
        def _(pe):
            def body(turn, first):
                for j in range(GROUP):
                    c = turn * GROUP + j
                    pe.wait_ge(arrived[j], turn * 16 + 16)
                    pe.wait_ge(ready, c * 3 + 3)
                    carried = not first or j >= 1
                    if not first or j >= 2:
                        pe.wait_ge(kept, (c - 1) * KEPT)
                    for half in range(2):
                        last = nc.tensor.matmul(ps[j % 2][:, half, 0:step], sel[:, j % 2, :],
                                                rows[:, j, half * step:(half + 1) * step], start=True, stop=not carried)
                    if carried:
                        pe.wait_ge(kept, c * KEPT)
                        for half in range(2):
                            last = nc.tensor.matmul(ps[j % 2][:, half, 0:step], car[:, j % 2, :],
                                                    sums[:, (j - 1) % GROUP, half * step:(half + 1) * step],
                                                    start=False, stop=True)
                    last.then_inc(summed, 1)
            groups(pe, body)

        @block.scalar
        def _(act):
            act.wait_ge(cleared, 3)

            def body(turn, first):
                for j in range(GROUP):
                    c = turn * GROUP + j
                    act.wait_ge(summed, c + 1)
                    if not first:
                        act.wait_ge(stored[j], turn * 16)
                    nc.scalar.activation(sums[:, j, 0:F].rearrange("p (a f) -> p a f", a=2), ps[j % 2][:, :, 0:step],
                                         ACT.Copy).then_inc(kept, 1)
                    if H:
                        own = g["own_w"][:, bass.ds(c, 1), 0:H].rearrange("p c h -> p (c h)")
                        nc.scalar.activation(sums[:, j, F:F + H], own, ACT.Copy).then_inc(kept, 1)
            groups(act, body)


def dense_pass(nc, g, tag, kind, a, out, scores=None, row=None, agg=None, res=None, weights=None, bias=None):
    H = {"project": 4, "attend": 4, "update": 2, "heads": 12, "conv": 0}[kind]
    S = {"project": KC, "attend": KC, "update": KC + 2, "heads": 2 * KC, "conv": KC}[kind]
    C = {"project": D + 8, "attend": 192 + 4}.get(kind, D)
    F = 192 if kind == "update" else D
    norm = kind in ("update", "heads") or (kind == "conv" and res is not None)
    split = kind != "heads"
    loads = []
    if row is not None:
        loads.append(("row", row, F))
    if agg is not None:
        loads.append(("agg", agg, F + H))
    if res is not None and res is not row:
        loads.append(("res", res, D))
    L = len(loads)
    OUT_W = {"project": D + 10, "attend": 197, "update": D + 25}.get(kind, D)
    cut = {"project": D, "attend": 192, "update": D}.get(kind, D)
    n_store = 2 if scores is not None else 1

    with ExitStack() as ctx:
        def sb(name, shape, dt=F32):
            return ctx.enter_context(nc.sbuf_tensor(f"{tag}_{name}", shape, dt))

        sem = semaphores(nc, ctx, f"{tag}_")

        ins = {name: sb(name, [P, UNROLL, w]) for name, _, w in loads}
        XW = {"update": 256}.get(kind, D)
        x = sb("x", [P, 2, XW])
        hi = sb("hi", [P, 2, S, P], F32R if split else F32)
        lo = sb("lo", [P, 2, S, P], F32R) if split else None
        outs = sb("outs", [P, UNROLL, OUT_W])
        y = sb("y", [P, 2, D])
        own_w = sb("own_w", [P, 2, 12])
        scrap = sb("scrap", [P, 1])
        stats, mv = sb("stats", [P, 2, 2, 6]), sb("mv", [P, 2, 2])
        root, rstd, shift = sb("root", [P, 2, 1]), sb("rstd", [P, 2, 1]), sb("shift", [P, 2, 1])
        if kind == "heads":
            w_st = sb("w_st", [P, 2, P])
        else:
            w_st = sb("w_st", [P, S, C])
            w_hi, w_lo = sb("w_hi", [P, S, C], F32R), sb("w_lo", [P, S, C], F32R)
        const = sb("const", [P, C])
        turned_ps = ctx.enter_context(nc.psum_tensor(f"{tag}_turned_ps", [P, -(-S // 4) * 4, P], F32))
        prods = [ctx.enter_context(nc.psum_tensor(f"{tag}_prod{i}", [P, 1 if C <= 512 else 2, 512], F32)) for i in range(2)]
        pieces = [(0, 0, C)] if C <= 512 else [(0, 0, HALF), (1, HALF, C)]

        loaded = [sem(f"loaded{j}") for j in range(UNROLL)]
        stored = [sem(f"stored{j}") for j in range(UNROLL)]
        w_in, w_made, w_const, w_rounded, w_ready = sem("w_in"), sem("w_made"), sem("w_const"), sem("w_rounded"), sem("w_ready")
        w_zero, built, turned, hi_done, split_done = sem("w_zero"), sem("built"), sem("turned"), sem("hi_done"), sem("split_done")
        multiplied, prod_read, polished, out_ready = sem("multiplied"), sem("prod_read"), sem("polished"), sem("out_ready")
        spread, rooted, shifted = sem("spread"), sem("rooted"), sem("shifted")
        prep_self, build_self, end_self, score_self = sem("prep_self"), sem("build_self"), sem("end_self"), sem("score_self")
        out_self = sem("out_self")
        block = ctx.enter_context(nc.Block())

        if kind == "project":
            heads_of, att = (4, 192), (a["L0_gnn_a_src1"], a["L0_gnn_a_dst1"])
        elif kind == "attend":
            heads_of, att = (2, 96), (a["L0_gnn_a_src2"], a["L0_gnn_a_dst2"])
        else:
            heads_of, att = None, ()
        if heads_of:
            att_b = sb("att_b", [P, 2, cut])
            scratch = sb("scratch", [P, S, cut])
            b_col = sb("b_col", [P, S])
        if kind == "project":
            g_col = sb("g_col", [P, S])
        if kind == "update":
            b_col = sb("b_col", [P, 2])
            bu_b = sb("bu_b", [P, D])
            w_fc = sb("w_fc", [64, 64])
            att_t = sb("att_t", [64, 2, 12])
            score_v = sb("score_v", [P, 2, D])
            marked = sb("marked", [P, D])
        N_W_IN = {"project": 5, "attend": 4, "update": 7, "heads": 4, "conv": 2}[kind]

        @block.sync
        def _(sp):
            wait_zero = kind in ("update", "heads")
            if wait_zero:
                sp.wait_ge(w_zero, 3 if kind == "update" else 1)

            def load_w(dst, src, scattered=False):
                sp.dma_start(dst, src, allow_slow_non_contiguous=scattered).then_inc(w_in, 16)
            if kind in ("project", "attend", "conv"):
                load_w(w_st[:, :, 0:cut], weights.rearrange("(s p) c -> p s c", p=P))
            if heads_of:
                load_w(att_b[:, 0, :], att[0].rearrange("h c -> (h c)").partition_broadcast(P))
                load_w(att_b[:, 1, :], att[1].rearrange("h c -> (h c)").partition_broadcast(P))
                load_w(b_col[:, :], bias.rearrange("(s p) -> p s", p=P), True)
            if kind == "project":
                load_w(g_col[:, :], a["L0_gnn_norm_g"].rearrange("(s p) -> p s", p=P), True)
            if kind == "update":
                full = D + P
                load_w(w_st[:, 0:KC + 1, :], weights[0:full, :].rearrange("(s p) c -> p s c", p=P))
                load_w(w_st[0:64, KC + 1, :], weights[full:full + 64, :])
                load_w(b_col[:, 0:1], bias[0:P].rearrange("(p o) -> p o", o=1), True)
                load_w(b_col[0:64, 1:2], bias[P:192].rearrange("(p o) -> p o", o=1), True)
                load_w(bu_b[:, :], a["L0_gnn_bu"].partition_broadcast(P))
                load_w(w_fc[:, :], a["L1_gnn_W_fc"])
                with nc.allow_non_contiguous_dma(reason="two small transposed loads"):
                    sp.dma_start(att_t[:, 0, :], a["L1_gnn_attn_l"].rearrange("h e -> e h")).then_inc(w_in, 16)
                    sp.dma_start(att_t[:, 1, :], a["L1_gnn_attn_r"].rearrange("h e -> e h")).then_inc(w_in, 16)
            if kind == "heads":
                with nc.allow_non_contiguous_dma(reason="small transposed loads"):
                    for k, w in enumerate((a["L1_gnn_W_fc"], a["L1_gnn_W_res"])):
                        for q in range(2):
                            sp.dma_start(w_st[64 * q:64 * q + 64, k, 64 * q:64 * q + 64],
                                         w.rearrange("e d -> d e")).then_inc(w_in, 16)
            if kind == "conv":
                load_w(const[:, :], bias.partition_broadcast(P))

            def load(t, slot, turn):
                if at_least(t, UNROLL):
                    sp.wait_ge(prod_read, t - UNROLL + 1)
                n = rows_of(t)
                for name, table, w in loads:
                    sp.dma_start(ins[name][0:n, slot, :], tile_rows(table, t)[:, 0:w]).then_inc(loaded[slot], 16)
            over_tiles(sp, load)

        @block.gpsimd
        def _(pool):
            if kind == "update":
                nc.gpsimd.memset(w_st[:, :, :], 0.0).then_inc(w_zero, 1)
                nc.gpsimd.memset(b_col[:, :], 0.0).then_inc(w_zero, 1)
                nc.gpsimd.memset(x[:, :, :], 0.0).then_inc(w_zero, 1)
                pool.wait_ge(w_zero, 3)
                nc.gpsimd.memset(x[:, :, 192:193], 1.0).then_inc(w_zero, 1)
            if kind == "heads":
                nc.gpsimd.memset(w_st[:, :, :], 0.0).then_inc(w_zero, 1)

            def store(t, slot, turn):
                pool.wait_ge(polished if kind in ("heads", "conv") else out_ready, t + 1)
                n = rows_of(t)
                nc.gpsimd.dma_start(tile_rows(out, t), outs[0:n, slot, 0:cut]).then_inc(stored[slot], 16)
                if scores is not None:
                    nc.gpsimd.dma_start(tile_rows(scores, t), outs[0:n, slot, cut:OUT_W]).then_inc(stored[slot], 16)
            over_tiles(pool, store)
            for j in range(UNROLL):
                pool.wait_ge(stored[j], 16 * n_store * ((NT - 1 - j) // UNROLL + 1))

        @block.vector
        def _(dve):
            v, n = nc.vector, [0]

            def link(ins_):
                n[0] += 1
                ins_.then_inc(prep_self, 1)
                dve.wait_ge(prep_self, n[0])

            if N_W_IN:
                dve.wait_ge(w_in, 16 * (8 if kind == "update" else N_W_IN))
            if heads_of:
                nh, width = heads_of
                for k in range(2):
                    link(v.tensor_tensor(scratch[:, :, :], w_st[:, :, 0:cut],
                                         att_b[:, k:k + 1, :].to_broadcast([P, S, cut]), ALU.mult))
                    for h in range(nh):
                        link(v.tensor_reduce(w_st[:, :, cut + k * nh + h], scratch[:, :, h * width:(h + 1) * width], AX.X, ALU.add))
                v.tensor_copy(scratch[:, 0, 0:1], b_col[:, 0:1]).then_inc(w_made, 1)
                dve.wait_ge(w_const, 1)
                if len(pieces) == 2:
                    link(v.tensor_copy(const[:, 0:HALF], prods[0][:, 0, 0:HALF]))
                    link(v.tensor_copy(const[:, HALF:C], prods[0][:, 1, 0:C - HALF]))
                else:
                    link(v.tensor_copy(const[:, :], prods[0][:, 0, 0:C]))
                if kind == "project":
                    link(v.tensor_tensor(w_st[:, :, :], w_st[:, :, :], g_col[:, :].unsqueeze(2).to_broadcast([P, S, C]), ALU.mult))
            if kind == "update":
                dve.wait_ge(w_zero, 4)
                dve.wait_ge(w_const, 1)
                cv = const[:, :].rearrange("p (a f) -> p a f", a=2)
                link(v.tensor_tensor(cv, prods[0][:, :, 0:HALF], bu_b[:, :].rearrange("p (a f) -> p a f", a=2), ALU.add))
                link(v.tensor_copy(w_st[64:65, KC + 1, :], const[64:65, :]))
                for k in range(2):
                    link(v.tensor_copy(score_v[:, k, 0:512], turned_ps[:, 0:4, :].rearrange("p s c -> p (s c)") if k == 0
                                       else prods[1][:, 0, :]))
                    link(v.tensor_copy(score_v[:, k, 512:D], turned_ps[:, 4:6, :].rearrange("p s c -> p (s c)") if k == 0
                                       else prods[1][:, 1, 0:D - 512]))
            if kind == "heads":
                v.tensor_copy(const[:, 0:1], w_st[:, 0, 0:1]).then_inc(w_ready, 1)
            else:
                v.tensor_copy(y[:, 0, 0:1], w_st[:, 0, 0:1]).then_inc(w_made, 1)
                dve.wait_ge(w_rounded, 1)
                v.tensor_tensor(w_lo[:, :, :], w_st[:, :, :], w_hi[:, :, :].bitcast(F32), ALU.subtract).then_inc(w_ready, 1)

            bc = Count(build_self, {"project": 2, "attend": 2, "update": 2, "heads": 2, "conv": 1}[kind])
            ec = Count(end_self, 0)
            ec.per = {"project": 2, "attend": 1, "update": 3, "heads": 3, "conv": 4 if norm else 1}[kind]
            rc = Count(score_self, 3)

            def stat(t, s2, src):
                c = bc if kind == "project" else ec
                v.bn_stats(stats[:, s2, 0, :], src[:, 0:HALF]).then_inc(c.sem, 1)
                c.n += 1
                c.link(dve, v.bn_stats(stats[:, s2, 1, :], src[:, HALF:D]))
                v.memset(scrap[:, :], 0.0)
                v.bn_aggr(mv[:, s2, :], stats[:, s2, :, :].rearrange("p a s -> p (a s)")).then_inc(spread, 1)

            def shift_of(t, s2):
                dve.wait_ge(rooted, t + 1)
                v.reciprocal(rstd[:, s2, :], root[:, s2, :]).then_inc(shifted, 1)
                dve.wait_ge(shifted, t * 2 + 1)
                v.scalar_tensor_tensor(shift[:, s2, :], mv[:, s2, 0:1], -1.0, rstd[:, s2, :], ALU.mult, ALU.mult).then_inc(shifted, 1)

            def build(t, slot, turn):
                s2 = slot % 2
                bc.step(t)
                dve.wait_ge(loaded[slot], turn * (16 * L) + 16 * L)
                if kind == "project":
                    stat(t, s2, ins["row"][:, slot, :])
                    if at_least(t, 2):
                        dve.wait_ge(built, t - 1)
                    shift_of(t, s2)
                    return
                if at_least(t, 2):
                    dve.wait_ge(turned, t - 1)
                r, ag = ins["row"][:, slot, :], ins["agg"][:, slot, 0:F]
                if kind == "conv":
                    bc.n += 1
                    v.scalar_tensor_tensor(x[:, s2, :], r, g["own_d"][:, bass.ds(t, 1)], ag, ALU.mult, ALU.add).then_inc(built, 1)
                    return
                extra = g["has_own"][:, bass.ds(t, 1)].to_broadcast([P, H]) if kind == "heads" else g["ones"][:, 0:H]
                bc.link(dve, v.tensor_tensor(own_w[:, s2, 0:H], ins["agg"][:, slot, F:F + H], extra, ALU.add))
                x3 = x[:, s2, 0:F].rearrange("p (h f) -> p h f", h=H)
                bc.link(dve, v.tensor_tensor(x3, r.rearrange("p (h f) -> p h f", h=H),
                                             own_w[:, s2, 0:H].unsqueeze(2).to_broadcast([P, H, F // H]), ALU.mult))
                v.tensor_tensor(x[:, s2, 0:F], x[:, s2, 0:F], ag, ALU.add).then_inc(built, 1)

            def low(t, slot, turn):
                dve.wait_ge(hi_done, t + 1)
                if at_least(t, 2):
                    dve.wait_ge(multiplied, t - 1)
                s2 = slot % 2
                v.tensor_tensor(lo[:, s2, :, :], turned_ps[:, 0:S, :], hi[:, s2, :, :].bitcast(F32), ALU.subtract).then_inc(split_done, 1)

            def end(t, slot, turn):
                s2 = slot % 2
                ec.step(t)
                pr = prods[s2]
                dve.wait_ge(multiplied, t + 1)
                if kind in ("project", "attend"):
                    if at_least(t, UNROLL):
                        dve.wait_ge(stored[slot], turn * (16 * n_store))
                    o = outs[:, slot, :]
                    if kind == "project":
                        ec.link(dve, v.tensor_tensor(o[:, 0:D].rearrange("p (a f) -> p a f", a=2), pr[:, :, 0:HALF],
                                                     const[:, 0:D].rearrange("p (a f) -> p a f", a=2), ALU.add))
                        ec.n += 1
                        v.tensor_tensor(o[:, D:C], pr[:, 1, HALF:C - HALF], const[:, D:C], ALU.add).then_inc(ec.sem, 1)
                        dve.wait_ge(ec.sem, ec.base + ec.n)
                        v.tensor_copy(o[:, C:OUT_W], g["node"][:, bass.ds(t * 2, 2)]).then_inc(out_ready, 1)
                    else:
                        ec.link(dve, v.tensor_tensor(o[:, 0:C], pr[:, 0, 0:C], const[:, :], ALU.add))
                        v.tensor_copy(o[:, C:OUT_W], g["node"][:, bass.ds(t * 2, 1)]).then_inc(out_ready, 1)
                    dve.sem_inc(prod_read, 1)
                    return
                if at_least(t, 2):
                    dve.wait_ge(polished, t - 1)
                ys = y[:, s2, :]
                y3, p3 = ys.rearrange("p (a f) -> p a f", a=2), pr[:, :, 0:HALF]
                if kind == "update":
                    ec.link(dve, v.tensor_tensor(y3, p3, ins["res"][:, slot, :].rearrange("p (a f) -> p a f", a=2), ALU.add))
                elif kind == "heads":
                    ec.link(dve, v.scalar_tensor_tensor(y3, p3, 0.0, ins["row"][:, slot, :].rearrange("p (a f) -> p a f", a=2),
                                                        ALU.max, ALU.add))
                else:
                    c3 = const[:, :].rearrange("p (a f) -> p a f", a=2)
                    if not norm:
                        ec.link(dve, v.scalar_tensor_tensor(y3, p3, g["dinv"][:, bass.ds(t, 1)], c3, ALU.mult, ALU.add))
                        dve.sem_inc(prod_read, 1)
                        dve.sem_inc(spread, 1)
                        return
                    r3 = ins["row" if res is row else "res"][:, slot, :].rearrange("p (a f) -> p a f", a=2)
                    ec.link(dve, v.scalar_tensor_tensor(y3, p3, g["dinv"][:, bass.ds(t, 1)], r3, ALU.mult, ALU.add))
                    ec.link(dve, v.tensor_tensor(ys, ys, const[:, :], ALU.add))
                dve.sem_inc(prod_read, 1)
                stat(t, s2, ys)

            def end2(t, slot, turn):
                if norm:
                    shift_of(t, slot % 2)

            def score(t, slot, turn):
                rc.step(t)
                dve.wait_ge(polished, t + 1)
                o = outs[:, slot, :]
                if at_least(t, 1):
                    dve.wait_ge(out_ready, t)
                for k in range(2):
                    rc.link(dve, v.tensor_tensor(marked[:, :], o[:, 0:D], score_v[:, k, :], ALU.mult))
                    red = v.tensor_reduce(o[:, D + 12 * k:D + 12 * k + 12], marked[:, :].rearrange("p (h f) -> p h f", h=12),
                                          AX.X, ALU.add)
                    if k == 0:
                        rc.link(dve, red)
                    else:
                        red.then_inc(out_self, 1)
                dve.wait_ge(out_self, t + 1)
                v.tensor_copy(o[:, D + 24:D + 25], g["own"][:, bass.ds(t, 1)]).then_inc(out_ready, 1)

            def step(t, slot, turn):
                if live(t):
                    build(t, slot, turn)
                b = back(t, slot, turn, 2)
                if at_least(t, 2) and live(b[0]):
                    end(*b)
                if live(t) and split:
                    low(t, slot, turn)
                if at_least(t, 2) and live(b[0]):
                    end2(*b)
                b = back(t, slot, turn, 3)
                if kind == "update" and at_least(t, 3) and live(b[0]):
                    score(*b)
            over_tiles(dve, step, 3 if kind == "update" else 2)

        @block.scalar
        def _(act):
            if kind != "heads":
                act.wait_ge(w_made, 2 if heads_of else 1)
                nc.scalar.activation(w_hi[:, :, :], w_st[:, :, :], ACT.Copy).then_inc(w_rounded, 1)

            def root_of(t, s2):
                act.wait_ge(spread, t + 1)
                nc.scalar.activation(root[:, s2, :], mv[:, s2, 1:2], ACT.Sqrt, bias=g["eps"][:, 0:1]).then_inc(rooted, 1)

            def step(t, slot, turn):
                s2 = slot % 2
                if live(t):
                    if kind == "project":
                        root_of(t, s2)
                        act.wait_ge(shifted, t * 2 + 2)
                        if at_least(t, 2):
                            act.wait_ge(turned, t - 1)
                        nc.scalar.activation(x[:, s2, :], ins["row"][:, slot, :], ACT.Identity, bias=shift[:, s2, :],
                                             scale=rstd[:, s2, :]).then_inc(built, 1)
                    act.wait_ge(turned, t + 1)
                    if at_least(t, 2):
                        act.wait_ge(multiplied, t - 1)
                    nc.scalar.activation(hi[:, s2, :, :], turned_ps[:, 0:S, :], ACT.Copy).then_inc(hi_done, 1)
                if kind in ("project", "attend") or not at_least(t, 2):
                    return
                t, slot, turn = back(t, slot, turn, 2)
                if not live(t):
                    return
                s2 = slot % 2
                if norm:
                    root_of(t, s2)
                    act.wait_ge(shifted, t * 2 + 2)
                else:
                    act.wait_ge(spread, t + 1)
                if at_least(t, UNROLL):
                    act.wait_ge(stored[slot], turn * (16 * n_store))
                inc = polished if kind == "update" else None
                if norm:
                    last = nc.scalar.activation(outs[:, slot, 0:D], y[:, s2, :], ACT.Identity, bias=shift[:, s2, :],
                                                scale=rstd[:, s2, :])
                else:
                    last = nc.scalar.activation(outs[:, slot, 0:D], y[:, s2, :], ACT.Relu)
                last.then_inc(polished, 1)
            over_tiles(act, step, 2)

        @block.tensor
        def _(pe):
            if heads_of:
                pe.wait_ge(w_made, 1)
                for bank, c0, c1 in pieces:
                    for k in range(S):
                        last = nc.tensor.matmul(prods[0][:, bank, 0:c1 - c0], b_col[:, k:k + 1].to_broadcast([P, P]),
                                                w_st[:, k, c0:c1], start=(k == 0), stop=(k == S - 1))
                last.then_inc(w_const, 1)
            if kind == "update":
                pe.wait_ge(w_in, 16 * 8)
                pe.wait_ge(w_zero, 4)
                for bank, c0, c1 in pieces:
                    for k in range(2):
                        nc.tensor.matmul(prods[0][:, bank, 0:c1 - c0], b_col[:, k:k + 1].to_broadcast([P, P]),
                                         w_st[:, KC + k, c0:c1], start=(k == 0), stop=(k == 1))
                for k in range(2):
                    for h in range(12):
                        o = turned_ps[:, h // 2, 64 * (h % 2):64 * (h % 2) + 64] if k == 0 else \
                            prods[1][:, h // 8, 64 * (h % 8):64 * (h % 8) + 64]
                        last = nc.tensor.matmul(o, att_t[:, k, h:h + 1].to_broadcast([64, P]), w_fc[:, :], start=True, stop=True)
                last.then_inc(w_const, 1)
            pe.wait_ge(w_ready, 1)

            def turn_over(t, slot, turn):
                pe.wait_ge(built, t + 1)
                if at_least(t, 1):
                    pe.wait_ge(split_done if split else hi_done, t)
                s2 = slot % 2
                for s in range(S):
                    if kind == "update":
                        src = ins["res"][:, slot, s * P:(s + 1) * P] if s < KC else x[:, s2, (s - KC) * P:(s - KC + 1) * P]
                    elif kind == "heads":
                        src = x[:, s2, s * P:(s + 1) * P] if s < KC else ins["row"][:, slot, (s - KC) * P:(s - KC + 1) * P]
                    else:
                        src = x[:, s2, s * P:(s + 1) * P]
                    last = nc.tensor.transpose(turned_ps[:, s, :], src, g["ident"][:, :])
                last.then_inc(turned, 1)

            def multiply(t, slot, turn):
                s2 = slot % 2
                pe.wait_ge(split_done if split else hi_done, t + 1)
                if at_least(t, 2):
                    pe.wait_ge(prod_read, t - 1)
                if kind == "heads":
                    for s in range(KC):
                        o = prods[s2][:, s // 3, (s % 3) * P:(s % 3 + 1) * P]
                        nc.tensor.matmul(o, hi[:, s2, s, :], w_st[:, 0, :], start=True, stop=False)
                        last = nc.tensor.matmul(o, hi[:, s2, KC + s, :], w_st[:, 1, :], start=False, stop=True)
                else:
                    for s in range(S):
                        terms = ((hi, w_hi), (hi, w_lo), (lo, w_hi))
                        for i, (l, w) in enumerate(terms):
                            for bank, c0, c1 in pieces:
                                last = nc.tensor.matmul(prods[s2][:, bank, 0:c1 - c0], l[:, s2, s, :], w[:, s, c0:c1],
                                                        start=(s == 0 and i == 0), stop=(s == S - 1 and i == 2))
                last.then_inc(multiplied, 1)

            def step(t, slot, turn):
                if live(t):
                    turn_over(t, slot, turn)
                b = back(t, slot, turn, 1)
                if at_least(t, 1) and live(b[0]):
                    multiply(*b)
            over_tiles(pe, step, 1)


_OUTS = [((N, D), "float32")]


def kernel(**inputs):
    import numpy as _np
    import concourse.bacc as _bacc
    from concourse import mybir as _mybir
    from concourse.bass_utils import run_bass_kernel_spmd as _run

    nc = _bacc.Bacc("TRN2", target_bir_lowering=False, num_devices=1)
    arrays, args = {}, {}
    for name in inputs:
        arr = _np.ascontiguousarray(inputs[name])
        arrays[f"in_{name}_dram"] = arr
        args[name] = nc.dram_tensor(f"in_{name}_dram", arr.shape, _mybir.dt.from_np(arr.dtype), kind="ExternalInput").ap()
    out = nc.dram_tensor("out_0_dram", _OUTS[0][0], _mybir.dt.float32, kind="ExternalOutput").ap()
    build(nc, args, out)
    r = _run(nc, [arrays], core_ids=[0])
    return r.results[0]["out_0_dram"]
```

```python
import concourse.bass as bass
from concourse import mybir
from concourse.alu_op_type import AluOpType as ALU
from contextlib import ExitStack

F32 = mybir.dt.float32
F32R = mybir.dt.float32r
BF16 = mybir.dt.bfloat16
I32 = mybir.dt.int32
ACT = mybir.ActivationFunctionType
AX = mybir.AxisListType

P = 128
N = 10000
E = 12500
D = 768
NT = (N + P - 1) // P
LAST_ROWS = N - (NT - 1) * P
GROUP = 4
NC = -(-E // (P * GROUP)) * GROUP
NG = NC // GROUP
BLOCK = 6
assert (NG - 1) % BLOCK == 0
EP, EC = 125, 100
FAR = 20000
NEG = 1e30
EPS = 1e-5
SLOPE = 0.2
KC = D // P
HALF = D // 2
H_MAX = 12
AGG_W = D + H_MAX
UNROLL = 4
assert EP * EC == E and NT % UNROLL == 3


class Count:

    def __init__(self, sem, per):
        self.sem, self.per = sem, per
        self.base, self.n = 0, 0

    def step(self, t):
        assert self.n in (0, self.per), (self.n, self.per)
        self.base, self.n = t * self.per, 0

    def link(self, eng, ins):
        self.n += 1
        ins.then_inc(self.sem, 1)
        eng.wait_ge(self.sem, self.base + self.n)


def semaphores(nc, ctx, prefix):
    held = []

    def give_back():
        nc.clear_and_free_semaphores(held)
        nc.all_engine_barrier()
    ctx.callback(give_back)

    def sem(name):
        held.append(nc.alloc_semaphore(prefix + name))
        return held[-1]
    return sem


def take_wait(nc, g, scrap):
    c = g["ones"][0:scrap.shape[0], 0:1]
    nc.gpsimd.tensor_tensor(scrap, c, c, ALU.add)


def at_least(t, k):
    return not isinstance(t, int) or t >= k


def over_tiles(eng, step, drain=0):
    for t in range(UNROLL):
        step(t, t, 0)
    with eng.Fori(1, NT // UNROLL) as i:
        for j in range(UNROLL):
            step(i * UNROLL + j, j, i)
    for t in range(NT // UNROLL * UNROLL, NT + drain):
        step(t, t % UNROLL, t // UNROLL)


def back(t, slot, turn, lag):
    return t - lag, (slot - lag) % UNROLL, turn + (slot - lag) // UNROLL


def live(t):
    return not isinstance(t, int) or 0 <= t < NT


def over_groups(eng, g, body):
    body(0, 0, 0)
    total = eng.value_load(g["total_i"][0:1, 0:1], min_val=0, max_val=E)
    with eng.Fori(0, (NG - 1) // BLOCK) as b:
        with eng.If(total > b * (BLOCK * GROUP * P) + GROUP * P):
            with eng.Fori(0, BLOCK // 2) as k:
                pair = b * (BLOCK // 2) + k
                for j in (1, 2):
                    with eng.If(total > pair * (2 * GROUP * P) + j * GROUP * P):
                        body(pair * 2 + j, j % 2, pair + j // 2)


def rows_of(t):
    return LAST_ROWS if isinstance(t, int) and t == NT - 1 else P


def tile_rows(ap, t):
    if isinstance(t, int):
        return ap[t * P:t * P + rows_of(t), :]
    return ap[bass.ds(t * P, P), :]


def build(nc, a, out):
    dram = lambda name, shape, dt=F32: nc.dram_tensor(name, shape, dt, kind="Internal").ap()
    packed = dram("packed", ((NC + 2) * P, 2))
    agg = dram("agg", (N, AGG_W))
    agg2 = dram("agg2", (N, 192 + 2))
    h1 = dram("h1", (N, D))
    sc1 = dram("sc1", (N, 10))
    h2 = dram("h2", (N, 192))
    sc2 = dram("sc2", (N, 5))
    x1 = dram("x1", (N, D))
    sc3 = dram("sc3", (N, 25))
    x2 = dram("x2", (N, D))
    x3 = dram("x3", (N, D))
    h3 = dram("h3", (N, D))

    with ExitStack() as ctx:
        def sb(name, shape, dt=F32):
            return ctx.enter_context(nc.sbuf_tensor(name, shape, dt))

        g = {
            "iota": sb("iota", [P, P]), "ident": sb("ident", [P, P]), "upper": sb("upper", [P, P]),
            "ones": sb("ones", [P, P]), "last_lane": sb("last_lane", [P, 1]), "eps": sb("eps", [P, 1]),
            "own": sb("own", [P, NT]), "dinv": sb("dinv", [P, NT]), "own1": sb("own1", [P, NT]),
            "own_d": sb("own_d", [P, NT]), "has_own": sb("has_own", [P, NT]),
            "src_i": sb("src_i", [P, NC + GROUP], I32), "dst_i": sb("dst_i", [P, NC + GROUP], I32), "put_i": sb("put_i", [P, NC], I32),
            "seg_end": sb("seg_end", [P, NC]), "carry_end": sb("carry_end", [P, NC]),
            "node": sb("node", [P, 2 * NT]),
            "total_i": sb("total_i", [P, 1], I32), "edge_dinv": sb("edge_dinv", [P, NC]),
            "same_f": sb("same_f", [NC, H_MAX * P]), "same_b": sb("same_b", [NC, H_MAX * P]),
            "pen_f": sb("pen_f", [NC, H_MAX * P]), "pen_b": sb("pen_b", [NC, H_MAX * P]),
            "cont_f": sb("cont_f", [NC, P]), "cont_b": sb("cont_b", [NC, P]),
            "row_f": sb("row_f", [H_MAX, NC]), "row_b": sb("row_b", [H_MAX, NC]),
            "alpha": sb("alpha", [P, NC, H_MAX]), "own_w": sb("own_w", [P, NC, H_MAX]),
        }
        prepare(nc, g, a, packed, agg, agg2)
        dense_pass(nc, g, "proj", "project", a, h1, sc1, row=a["x"], weights=a["L0_gnn_W1"], bias=a["L0_gnn_norm_b"])
        attention(nc, g, "l0a", 4, sc1, 10, 8, 9)
        gather_sum(nc, g, "l0a", h1, D, 4, agg)
        dense_pass(nc, g, "att", "attend", a, h2, sc2, row=h1, agg=agg, weights=a["L0_gnn_W2"], bias=a["L0_gnn_b1"])
        attention(nc, g, "l0b", 2, sc2, 5, 4, None)
        gather_sum(nc, g, "l0b", h2, 192, 2, agg2)
        dense_pass(nc, g, "upd", "update", a, x1, sc3, row=h2, agg=agg2, res=a["x"], weights=a["L0_gnn_Wu"], bias=a["L0_gnn_b2"])
        attention(nc, g, "l1", 12, sc3, 25, 24, None)
        gather_sum(nc, g, "l1", x1, D, 12, agg)
        dense_pass(nc, g, "hds", "heads", a, x2, row=x1, agg=agg)
        gather_sum(nc, g, "l2", x2, D, 0, agg)
        dense_pass(nc, g, "cv2", "conv", a, x3, row=x2, agg=agg, res=x2, weights=a["L2_gnn_W"], bias=a["L2_gnn_b"])
        gather_sum(nc, g, "l3a", x3, D, 0, agg)
        dense_pass(nc, g, "c3a", "conv", a, h3, row=x3, agg=agg, weights=a["L3_gnn_W1"], bias=a["L3_gnn_b1"])
        gather_sum(nc, g, "l3b", h3, D, 0, agg)
        dense_pass(nc, g, "c3b", "conv", a, out, row=h3, agg=agg, res=x3, weights=a["L3_gnn_W2"], bias=a["L3_gnn_b2"])


def prepare(nc, g, a, packed, agg, agg2):
    with ExitStack() as ctx:
        def sb(name, shape, dt=F32):
            return ctx.enter_context(nc.sbuf_tensor("pr_" + name, shape, dt))

        sem = semaphores(nc, ctx, "pr_")

        s_i, d_i = sb("s_i", [EP, EC], I32), sb("d_i", [EP, EC], I32)
        hi_i, lo_i = sb("hi_i", [EP, EC], I32), sb("lo_i", [EP, EC], I32)
        hi_f, lo_f = sb("hi_f", [EP, EC]), sb("lo_f", [EP, EC])
        rec = sb("rec", [EP, EC, 2])
        diff, same = sb("diff", [EP, EC]), sb("same", [EP, EC])
        rank, zero = sb("rank", [EP, EC]), sb("zero", [EP, EC])
        rank_i = sb("rank_i", [EP, EC], I32)
        before = sb("before", [P, P])
        scrap = sb("scrap", [P, 1])
        ix4, rec4 = sb("ix4", [EP, GROUP], I32), sb("rec4", [EP, GROUP, 2])
        lo_hot = sb("lo_hot", [EP, EC * P], BF16)
        hi_hot = sb("hi_hot", [EP, EC * 2 * NT], BF16)
        lo_hot3 = lo_hot[:, :].rearrange("p (c j) -> p c j", c=EC)
        hi_hot4 = hi_hot[:, :].rearrange("p (c k t) -> p c k t", c=EC, k=2)
        pad = sb("pad", [P, (NC + 2) * 2])
        zrow = sb("zrow", [P, AGG_W])
        sd_c = sb("sd_c", [P, NC, 2])
        sd_r = sb("sd_r", [NC, P, 2])
        prv, nxt = sb("prv", [NC, 1]), sb("nxt", [NC, 1])
        is_last, end_r = sb("is_last", [NC, P]), sb("end_r", [NC, P])
        val, carry_r = sb("val", [NC, P]), sb("carry_r", [NC, 1])
        last_c, tmp_c = sb("last_c", [P, NC]), sb("tmp_c", [P, NC])
        deg, sq = sb("deg", [P, NT]), sb("sq", [P, NT])
        all_f, all_b = sb("all_f", [NC, 1]), sb("all_b", [NC, 1])
        ps = ctx.enter_context(nc.psum_tensor("pr_ps", [P, 2 * NT], F32))
        ps2 = ctx.enter_context(nc.psum_tensor("pr_ps2", [P, 512], F32))
        ps3 = ctx.enter_context(nc.psum_tensor("pr_ps3", [P, 512], F32))

        loaded, consts, hots, hist = sem("loaded"), sem("consts"), sem("hots"), sem("hist")
        dve_self, pads, packs, zeros = sem("dve_self"), sem("pads"), sem("packs"), sem("zeros")
        slots = sem("slots")
        ranks, padded, counted, offset = sem("ranks"), sem("padded"), sem("counted"), sem("offset")
        reloaded, rooted, rows_done, turned = sem("reloaded"), sem("rooted"), sem("rows_done"), sem("turned")
        block = ctx.enter_context(nc.Block())

        @block.sync
        def _(sp):
            sp.dma_start(s_i[:, :], a["src"].rearrange("(p c) -> p c", p=EP)).then_inc(loaded, 16)
            sp.dma_start(d_i[:, :], a["dst"].rearrange("(p c) -> p c", p=EP)).then_inc(loaded, 16)
            sp.wait_ge(pads, 1)
            sp.dma_start(packed.rearrange("(p c) w -> p (c w)", p=P), pad[:, :]).then_inc(padded, 16)
            sp.wait_ge(pads, 2)

            def clear(t, slot, turn):
                sp.dma_start(tile_rows(agg, t), zrow[0:rows_of(t), :]).then_inc(zeros, 16)
                sp.dma_start(tile_rows(agg2, t), zrow[0:rows_of(t), 0:194]).then_inc(zeros, 16)
            over_tiles(sp, clear)
            sp.wait_ge(packs, 16 * EC)
            sp.dma_start(sd_c[:, :, :], packed[P:P + NC * P, :].rearrange("(c p) w -> p c w", p=P)).then_inc(reloaded, 16)
            sp.dma_start(sd_r[:, :, :], packed[P:P + NC * P, :].rearrange("(c j) w -> c j w", j=P)).then_inc(reloaded, 16)
            sp.dma_start(prv[:, :], packed.rearrange("(c j) w -> c j w", j=P)[0:NC, P - 1, 1:2],
                         allow_slow_non_contiguous=True).then_inc(reloaded, 16)
            sp.dma_start(nxt[:, :], packed.rearrange("(c j) w -> c j w", j=P)[2:NC + 2, 0, 1:2],
                         allow_slow_non_contiguous=True).then_inc(reloaded, 16)
            sp.wait_ge(zeros, 32 * NT)

        @block.gpsimd
        def _(pool):
            nc.gpsimd.memset(pad[:, :], float(FAR)).then_inc(pads, 1)
            nc.gpsimd.memset(zrow[:, :], 0.0).then_inc(pads, 1)
            nc.gpsimd.iota(g["iota"][:, :], [[1, P]], base=0, channel_multiplier=0,
                           allow_small_or_imprecise_dtypes=True).then_inc(consts, 1)
            nc.gpsimd.memset(g["ones"][:, :], 1.0).then_inc(consts, 1)
            nc.gpsimd.memset(g["ident"][:, :], 0.0).then_inc(consts, 1)
            nc.gpsimd.memset(g["eps"][:, :], EPS).then_inc(consts, 1)
            nc.gpsimd.memset(g["last_lane"][:, :], 0.0).then_inc(consts, 1)
            nc.gpsimd.memset(g["alpha"][:, :, :], 0.0).then_inc(consts, 1)
            nc.gpsimd.memset(g["own_w"][:, :, :], 0.0).then_inc(consts, 1)
            pool.wait_ge(consts, 7)
            nc.gpsimd.affine_select(out=g["ident"][:, :], in_=g["ident"][:, :], compare_op=ALU.not_equal, fill=1.0,
                                    base=0, pattern=[[-1, P]], channel_multiplier=1).then_inc(consts, 1)
            nc.gpsimd.affine_select(out=g["upper"][:, :], in_=g["ones"][:, :], compare_op=ALU.is_ge, fill=0.0,
                                    base=0, pattern=[[1, P]], channel_multiplier=-1).then_inc(consts, 1)
            nc.gpsimd.affine_select(out=before[:, :], in_=g["ones"][:, :], compare_op=ALU.is_ge, fill=0.0,
                                    base=-1, pattern=[[1, P]], channel_multiplier=-1).then_inc(consts, 1)
            nc.gpsimd.affine_select(out=g["last_lane"][:, :], in_=g["last_lane"][:, :], compare_op=ALU.not_equal,
                                    fill=1.0, base=-(P - 1), pattern=[[0, 1]], channel_multiplier=1).then_inc(consts, 1)
            pool.wait_ge(padded, 16)
            pool.wait_ge(ranks, 1)

            bound = pool.to_reg((NC + 2) * P - 1)

            def place(first, turn):
                if first:
                    pool.wait_ge(packs, turn * (16 * GROUP))
                nc.gpsimd.tensor_copy(ix4[:, :], rank_i[:, bass.ds(turn * GROUP, GROUP)]).then_inc(slots, 1)
                nc.gpsimd.tensor_copy(rec4[:, :, :], rec[:, bass.ds(turn * GROUP, GROUP), :]).then_inc(slots, 1)
                pool.wait_ge(slots, turn * 2 + 2)
                take_wait(nc, g, scrap[:, 0:1])
                for j in range(GROUP):
                    nc.gpsimd.indirect_dma_start(packed, bass.IndirectOffsetOnAxis(ap=ix4[:, j:j + 1], axis=0),
                                                 rec4[:, j, :], None, bounds_check=bound,
                                                 oob_is_err=False).then_inc(packs, 16)
            place(False, 0)
            with pool.Fori(1, EC // GROUP) as i:
                place(True, i)
            pool.wait_ge(packs, 16 * EC)

        @block.vector
        def _(dve):
            v, n = nc.vector, [0]

            def link(ins):
                n[0] += 1
                ins.then_inc(dve_self, 1)
                dve.wait_ge(dve_self, n[0])

            dve.wait_ge(consts, 11)
            dve.wait_ge(loaded, 32)
            link(v.memset(zero[:, :], 0.0))
            link(v.tensor_copy(rec[:, :, 0], s_i[:, :]))
            link(v.tensor_copy(rec[:, :, 1], d_i[:, :]))
            link(v.tensor_tensor(diff[:, :], rec[:, :, 0], rec[:, :, 1], ALU.not_equal))
            link(v.tensor_tensor(same[:, :], rec[:, :, 0], rec[:, :, 1], ALU.is_equal))
            v.tensor_tensor_scan(rank[:, :], diff[:, :], zero[:, :], 0.0, ALU.add, ALU.add).then_inc(counted, 1)
            link(v.tensor_scalar(hi_i[:, :], d_i[:, :], 7, None, ALU.arith_shift_right))
            link(v.tensor_scalar(lo_i[:, :], d_i[:, :], P - 1, None, ALU.bitwise_and))
            link(v.tensor_copy(hi_f[:, :], hi_i[:, :]))
            link(v.tensor_copy(lo_f[:, :], lo_i[:, :]))
            dve.wait_ge(offset, 1)
            link(v.tensor_scalar(rank[:, :], rank[:, :], ps2[0:EP, 0:1], float(P - 1 - FAR), ALU.add, ALU.add))
            link(v.tensor_tensor(rank[:, :], rank[:, :], diff[:, :], ALU.mult))
            link(v.tensor_scalar(rank[:, :], rank[:, :], float(FAR), None, ALU.add))
            v.tensor_copy(rank_i[:, :], rank[:, :]).then_inc(ranks, 1)
            link(v.tensor_copy(g["total_i"][:, :], ps2[:, 1:2]))
            lo_b = lo_f[:, :].unsqueeze(2).to_broadcast([EP, EC, P])
            hi_b = hi_f[:, :].unsqueeze(2).to_broadcast([EP, EC, NT])
            same_b = same[:, :].unsqueeze(2).to_broadcast([EP, EC, NT])
            iota_p = g["iota"][0:EP, :].unsqueeze(1).to_broadcast([EP, EC, P])
            iota_t = g["iota"][0:EP, 0:NT].unsqueeze(1).to_broadcast([EP, EC, NT])
            link(v.tensor_tensor(lo_hot3, lo_b, iota_p, ALU.is_equal))
            link(v.tensor_tensor(hi_hot4[:, :, 0, :], hi_b, iota_t, ALU.is_equal))
            v.tensor_tensor(hi_hot4[:, :, 1, :], hi_hot4[:, :, 0, :], same_b, ALU.mult).then_inc(hots, 1)
            dve.wait_ge(hist, 1)
            link(v.tensor_scalar(deg[:, :], ps[:, 0:NT], 1.0, None, ALU.add))
            link(v.tensor_copy(g["own"][:, :], ps[:, NT:2 * NT]))
            v.tensor_scalar(g["own1"][:, :], g["own"][:, :], 1.0, None, ALU.add).then_inc(rows_done, 1)
            link(v.tensor_scalar(g["has_own"][:, :], g["own"][:, :], 1.0, None, ALU.min))
            dve.wait_ge(rooted, 1)
            link(v.reciprocal(g["dinv"][:, :], sq[:, :]))
            link(v.tensor_tensor(g["own_d"][:, :], g["own1"][:, :], g["dinv"][:, :], ALU.mult))
            node = g["node"][:, :].rearrange("p (t k) -> p t k", k=2)
            link(v.tensor_copy(node[:, :, 0], g["own1"][:, :]))
            link(v.tensor_copy(node[:, :, 1], g["dinv"][:, :]))
            dve.wait_ge(reloaded, 64)
            dst = sd_r[:, :, 1]
            H = H_MAX
            f3 = g["same_f"][:, :].rearrange("c (h j) -> c h j", h=H)
            b3 = g["same_b"][:, :].rearrange("c (h j) -> c h j", h=H)
            link(v.memset(f3, 0.0))
            link(v.memset(b3, 0.0))
            link(v.tensor_tensor(f3[:, 0, 1:P], sd_r[:, 1:P, 1], sd_r[:, 0:P - 1, 1], ALU.is_equal))
            link(v.tensor_copy(b3[:, 0, 0:P - 1], f3[:, 0, 1:P]))
            link(v.tensor_copy(f3[:, 1:H, :], f3[:, 0, :].unsqueeze(1).to_broadcast([NC, H - 1, P])))
            link(v.tensor_copy(b3[:, 1:H, :], b3[:, 0, :].unsqueeze(1).to_broadcast([NC, H - 1, P])))
            link(v.tensor_scalar(g["pen_f"][:, :], g["same_f"][:, :], -1.0, NEG, ALU.add, ALU.mult))
            link(v.tensor_scalar(g["pen_b"][:, :], g["same_b"][:, :], -1.0, NEG, ALU.add, ALU.mult))
            link(v.tensor_tensor(g["cont_f"][:, :], dst, prv[:, :].to_broadcast([NC, P]), ALU.is_equal))
            link(v.tensor_tensor(g["cont_b"][:, :], dst, nxt[:, :].to_broadcast([NC, P]), ALU.is_equal))
            link(v.tensor_copy(all_f[:, :], g["cont_f"][:, P - 1:P]))
            v.tensor_copy(all_b[:, :], g["cont_b"][:, 0:1]).then_inc(rows_done, 1)
            link(v.tensor_copy(is_last[:, 0:P - 1], b3[:, 0, 0:P - 1]))
            link(v.tensor_copy(is_last[:, P - 1:P], g["cont_b"][:, P - 1:P]))
            link(v.tensor_scalar(is_last[:, :], is_last[:, :], -1.0, 1.0, ALU.mult, ALU.add))
            link(v.tensor_scalar(val[:, :], b3[:, 0, :], float(FAR), None, ALU.mult))
            link(v.tensor_tensor(val[:, :], val[:, :], g["iota"][0:NC, :], ALU.add))
            link(v.tensor_tensor_scan(end_r[:, ::-1], val[:, ::-1], val[:, ::-1], float(FAR), ALU.min, ALU.min))
            link(v.tensor_scalar(carry_r[:, :], end_r[:, 0:1], 1.0, None, ALU.add))
            link(v.tensor_tensor(carry_r[:, :], carry_r[:, :], g["cont_f"][:, 0:1], ALU.mult))
            v.tensor_scalar(carry_r[:, :], carry_r[:, :], -1.0, None, ALU.add).then_inc(rows_done, 1)
            dve.wait_ge(turned, 1)
            link(v.tensor_copy(g["row_f"][:, :], ps3[0:H, 0:NC]))
            link(v.tensor_copy(g["row_b"][:, :], ps3[0:H, 128:128 + NC]))
            link(v.tensor_copy(g["carry_end"][:, :], ps3[:, 256:256 + NC]))
            link(v.tensor_copy(g["seg_end"][:, :], ps2[:, 128:128 + NC]))
            link(v.tensor_copy(last_c[:, :], ps2[:, 256:256 + NC]))
            link(v.memset(g["src_i"][:, NC:], FAR))
            link(v.memset(g["dst_i"][:, NC:], FAR))
            link(v.tensor_copy(g["src_i"][:, 0:NC], sd_c[:, :, 0]))
            link(v.tensor_copy(g["dst_i"][:, 0:NC], sd_c[:, :, 1]))
            link(v.tensor_scalar(tmp_c[:, :], sd_c[:, :, 1], -float(FAR), None, ALU.add))
            link(v.tensor_tensor(tmp_c[:, :], tmp_c[:, :], last_c[:, :], ALU.mult))
            link(v.tensor_scalar(tmp_c[:, :], tmp_c[:, :], float(FAR), None, ALU.add))
            link(v.tensor_copy(g["put_i"][:, :], tmp_c[:, :]))

        @block.scalar
        def _(act):
            act.wait_ge(rows_done, 1)
            nc.scalar.activation(sq[:, :], deg[:, :], ACT.Sqrt).then_inc(rooted, 1)

        @block.tensor
        def _(pe):
            pe.wait_ge(consts, 11)
            pe.wait_ge(counted, 1)
            nc.tensor.matmul(ps2[0:EP, 0:1], before[0:EP, 0:EP], rank[:, EC - 1:EC], start=True, stop=True)
            nc.tensor.matmul(ps2[:, 1:2], g["ones"][0:EP, :], rank[:, EC - 1:EC], start=True, stop=True).then_inc(offset, 1)
            pe.wait_ge(hots, 1)

            def count(c, start, stop):
                return nc.tensor.matmul(ps[:, :], lo_hot[:, bass.ds(c * P, P)], hi_hot[:, bass.ds(c * 2 * NT, 2 * NT)],
                                        start=start, stop=stop, skip_group_check=True)
            count(0, True, False)
            with pe.Fori(1, EC - 1) as c:
                count(c, False, False)
            count(EC - 1, False, True).then_inc(hist, 1)
            pe.wait_ge(rows_done, 3)
            ident = g["ident"][0:NC, 0:NC]
            nc.tensor.matmul(ps3[0:H_MAX, 0:NC], all_f[:, :].to_broadcast([NC, H_MAX]), ident, start=True, stop=True)
            nc.tensor.matmul(ps3[0:H_MAX, 128:128 + NC], all_b[:, :].to_broadcast([NC, H_MAX]), ident, start=True, stop=True)
            nc.tensor.matmul(ps3[:, 256:256 + NC], carry_r[:, :].to_broadcast([NC, P]), ident, start=True, stop=True)
            nc.tensor.transpose(ps2[:, 128:128 + NC], end_r[:, :], ident)
            nc.tensor.transpose(ps2[:, 256:256 + NC], is_last[:, :], ident).then_inc(turned, 1)


def attention(nc, g, tag, H, scores, W, own_col, dinv_col):
    with ExitStack() as ctx:
        def sb(name, shape, dt=F32):
            return ctx.enter_context(nc.sbuf_tensor(f"{tag}_{name}", shape, dt))

        sem = semaphores(nc, ctx, f"{tag}_")

        from_src, from_dst = sb("from_src", [P, NC, W]), sb("from_dst", [P, NC, W])
        z, zo = sb("z", [P, H, NC]), sb("zo", [P, H, NC])
        got = sb("got", [P, 2, 2, GROUP, W])
        scrap = sb("scrap", [P, 1])
        ix = sb("ix", [P, 2, 2, GROUP], I32)
        z_edge = sb("z_edge", [H, NC])
        cpen = sb("cpen", [NC, P])
        own_c = sb("own_c", [P, NC])
        t0, t1 = sb("t0", [P, H, NC]), sb("t1", [P, H, NC])
        R = lambda name: sb(name, [NC, H * P])
        zr, zor, fwd, bwd, top, w, wo, w_tmp = R("zr"), R("zor"), R("fwd"), R("bwd"), R("top"), R("w"), R("wo"), R("w_tmp")
        own_r = sb("own_r", [NC, P])
        edge, edge_t = sb("edge", [NC, H]), sb("edge_t", [H, NC + 2])
        rows = sb("rows", [H, NC])
        psz = ctx.enter_context(nc.psum_tensor(f"{tag}_psz", [P, 2048], F32))
        pst = ctx.enter_context(nc.psum_tensor(f"{tag}_pst", [P, 512], F32))
        psb = ctx.enter_context(nc.psum_tensor(f"{tag}_psb", [P, 512], F32))
        zeroed, scored, turned = sem("zeroed"), sem("scored"), sem("turned")
        gathered = [sem(f"gathered{par}") for par in range(2)]
        dve_self, edges, edges_up, carries, carries_up = (sem("dve_self"), sem("edges"), sem("edges_up"),
                                                          sem("carries"), sem("carries_up"))
        indexed, copied = sem("indexed"), sem("copied")
        shifted, expd, back, freed = sem("shifted"), sem("expd"), sem("back"), sem("freed")
        block = ctx.enter_context(nc.Block())
        HW = H * P
        per_bank = 4

        @block.gpsimd
        def _(pool):
            nc.gpsimd.memset(from_src[:, :, :], 0.0).then_inc(zeroed, 1)
            nc.gpsimd.memset(from_dst[:, :, :], 0.0).then_inc(zeroed, 1)
            nc.gpsimd.memset(got[:, :, :, :, :], 0.0).then_inc(zeroed, 1)
            nc.gpsimd.memset(ix[:, :, :, :], 0).then_inc(zeroed, 1)
            pool.wait_ge(zeroed, 4)

            def fetch(turn, par):
                nc.gpsimd.tensor_copy(ix[:, par, 0, :], g["src_i"][:, bass.ds(turn * GROUP, GROUP)]).then_inc(indexed, 1)
                nc.gpsimd.tensor_copy(ix[:, par, 1, :], g["dst_i"][:, bass.ds(turn * GROUP, GROUP)]).then_inc(indexed, 1)
                pool.wait_ge(indexed, turn * 2 + 2)
                take_wait(nc, g, scrap[:, 0:1])
                for k in range(2):
                    for j in range(GROUP):
                        nc.gpsimd.indirect_dma_start(got[:, par, k, j, :], None, scores,
                                                     bass.IndirectOffsetOnAxis(ap=ix[:, par, k, j:j + 1], axis=0),
                                                     bounds_check=N - 1, oob_is_err=False).then_inc(gathered[par], 16)

            def body(turn, par, half):
                if at_least(turn, 1):
                    pool.wait_ge(copied, turn * 2)
                fetch(turn + 1, 1 - par)
                pool.wait_ge(gathered[1 - par], half * (32 * GROUP) + (32 * GROUP if par == 0 else 64 * GROUP))
            fetch(0, 0)
            over_groups(pool, g, body)

        @block.vector
        def _(dve):
            v, n = nc.vector, [0]

            def link(ins):
                n[0] += 1
                ins.then_inc(dve_self, 1)
                dve.wait_ge(dve_self, n[0])

            def take(turn, par, half):
                dve.wait_ge(gathered[par], half * (32 * GROUP) + 32 * GROUP)
                v.tensor_copy(from_src[:, bass.ds(turn * GROUP, GROUP), :], got[:, par, 0, :, :]).then_inc(copied, 1)
                v.tensor_copy(from_dst[:, bass.ds(turn * GROUP, GROUP), :], got[:, par, 1, :, :]).then_inc(copied, 1)
            dve.wait_ge(zeroed, 4)
            over_groups(dve, g, take)
            link(v.memset(z_edge[:, :], 0.0))
            ssrc = from_src[:, :, 0:H].rearrange("p c h -> p h c")
            sdst = from_dst[:, :, H:2 * H].rearrange("p c h -> p h c")
            osrc = from_dst[:, :, 0:H].rearrange("p c h -> p h c")
            if dinv_col is not None:
                link(v.tensor_copy(g["edge_dinv"][:, :], from_src[:, :, dinv_col]))
            link(v.tensor_copy(own_c[:, :], from_dst[:, :, own_col]))
            for x, y, dst in ((ssrc, sdst, z), (osrc, sdst, zo)):
                link(v.tensor_tensor(t0[:, :, :], x, y, ALU.add))
                link(v.scalar_tensor_tensor(dst[:, :, :], t0[:, :, :], SLOPE, t0[:, :, :], ALU.mult, ALU.max))
            link(v.tensor_scalar(t1[:, 0, :], own_c[:, :], 1.0, -1.0, ALU.min, ALU.add))
            link(v.tensor_scalar(t1[:, 0, :], t1[:, 0, :], NEG, None, ALU.mult))
            v.tensor_tensor(zo[:, :, :], zo[:, :, :], t1[:, 0:1, :].to_broadcast([P, H, NC]), ALU.add).then_inc(scored, 1)
            dve.wait_ge(turned, 1)
            link(v.tensor_copy(own_r[:, :], psb[0:NC, 0:P]))
            v.tensor_copy(zr[:, :], psz[0:NC, 0:HW]).then_inc(freed, 1)
            dve.wait_ge(turned, 2)
            link(v.tensor_copy(zor[:, :], psz[0:NC, 0:HW]))

            k = [0]

            def total_of(vals, into, forward, is_max):
                same = g[("pen_" if is_max else "same_") + ("f" if forward else "b")][:, 0:HW]
                cont = g["cont_f" if forward else "cont_b"]
                whole = g["row_f" if forward else "row_b"][0:H, :]
                none, op = (-NEG, ALU.max) if is_max else (0.0, ALU.add)
                hold = ALU.add if is_max else ALU.mult
                turn = (lambda x: x) if forward else (lambda x: x[:, ::-1])
                link(v.tensor_tensor_scan(turn(into[:, :]), turn(same), turn(vals[:, :]), none, hold, op))
                col = into[:, :].rearrange("c (h j) -> c h j", h=H)[:, :, P - 1 if forward else 0]
                v.tensor_copy(edge[:, :], col).then_inc(edges, 1)
                k[0] += 1
                dve.wait_ge(edges_up, k[0])
                src = pst[0:H, 0:NC]
                link(v.memset(edge_t[:, :], none))
                if is_max:
                    link(v.tensor_scalar(rows[:, :], whole, -1.0, NEG, ALU.add, ALU.mult))
                else:
                    link(v.tensor_copy(rows[:, :], whole))
                link(v.tensor_copy(z_edge[0:H, :], src))
                link(v.tensor_tensor_scan(turn(edge_t[:, 1:NC + 1]), turn(rows[:, :]), turn(z_edge[0:H, :]), none, hold, op))
                v.tensor_copy(z_edge[0:H, :], edge_t[:, 0:NC] if forward else edge_t[:, 2:NC + 2]).then_inc(carries, 1)
                dve.wait_ge(carries_up, k[0])
                i3 = into[:, :].rearrange("c (h j) -> c h j", h=H)
                x3 = w_tmp[:, :].rearrange("c (h j) -> c h j", h=H)
                cb = cont[:, :].unsqueeze(1).to_broadcast([NC, H, P])
                hand = pst[0:NC, 128:128 + H].unsqueeze(2).to_broadcast([NC, H, P])
                if is_max:
                    link(v.tensor_scalar(cpen[:, :], cont[:, :], -1.0, NEG, ALU.add, ALU.mult))
                    link(v.tensor_tensor(x3, hand, cpen[:, :].unsqueeze(1).to_broadcast([NC, H, P]), ALU.add))
                else:
                    link(v.tensor_tensor(x3, hand, cb, ALU.mult))
                link(v.tensor_tensor(into[:, :], into[:, :], w_tmp[:, :], op))

            total_of(zr, fwd, True, True)
            total_of(zr, bwd, False, True)
            link(v.tensor_tensor(top[:, :], fwd[:, :], bwd[:, :], ALU.max))
            link(v.tensor_tensor(top[:, :], top[:, :], zor[:, :], ALU.max))
            link(v.tensor_tensor(zr[:, :], zr[:, :], top[:, :], ALU.subtract))
            v.tensor_tensor(zor[:, :], zor[:, :], top[:, :], ALU.subtract).then_inc(shifted, 1)
            dve.wait_ge(expd, 2)
            wo3 = wo[:, :].rearrange("c (h j) -> c h j", h=H)
            ob = own_r[:, :].unsqueeze(1).to_broadcast([NC, H, P])
            link(v.tensor_tensor(wo3, wo3, ob, ALU.mult))
            total_of(w, fwd, True, False)
            total_of(w, bwd, False, False)
            link(v.tensor_tensor(top[:, :], fwd[:, :], bwd[:, :], ALU.add))
            link(v.tensor_tensor(top[:, :], top[:, :], w[:, :], ALU.subtract))
            link(v.tensor_tensor(top[:, :], top[:, :], wo[:, :], ALU.add))
            link(v.reciprocal(fwd[:, :], top[:, :]))
            link(v.tensor_tensor(w[:, :], w[:, :], fwd[:, :], ALU.mult))
            v.tensor_tensor(wo[:, :], wo[:, :], fwd[:, :], ALU.mult).then_inc(back, 1)
            for m, dst in ((1, "alpha"), (2, "own_w")):
                dve.wait_ge(turned, 2 + m)
                ph = psz[:, 0:HW].rearrange("p (h c) -> p c h", h=H)[:, 0:NC, :]
                if m == 1:
                    v.tensor_copy(g[dst][:, :, 0:H], ph).then_inc(freed, 1)
                else:
                    link(v.tensor_scalar(t1[:, 0, :], own_c[:, :], 1.0, None, ALU.min))
                    link(v.tensor_tensor(g[dst][:, :, 0:H], ph,
                                         t1[:, 0, :].unsqueeze(2).to_broadcast([P, NC, H]), ALU.subtract))

        @block.scalar
        def _(act):
            act.wait_ge(shifted, 1)
            nc.scalar.activation(w[:, :], zr[:, :], ACT.Exp).then_inc(expd, 1)
            nc.scalar.activation(wo[:, :], zor[:, :], ACT.Exp).then_inc(expd, 1)

        @block.tensor
        def _(pe):
            pe.wait_ge(scored, 1)
            for h in range(H):
                nc.tensor.transpose(psz[0:NC, h * P:(h + 1) * P], z[:, h, :], g["ident"][:, :])
            nc.tensor.transpose(psb[0:NC, 0:P], own_c[:, :], g["ident"][:, :]).then_inc(turned, 1)
            pe.wait_ge(freed, 1)
            for h in range(H):
                last = nc.tensor.transpose(psz[0:NC, h * P:(h + 1) * P], zo[:, h, :], g["ident"][:, :])
            last.then_inc(turned, 1)
            for k in range(1, 5):
                pe.wait_ge(edges, k)
                nc.tensor.transpose(pst[0:H, 0:NC], edge[:, :], g["ident"][0:NC, 0:NC]).then_inc(edges_up, 1)
                pe.wait_ge(carries, k)
                nc.tensor.transpose(pst[0:NC, 128:128 + H], z_edge[0:H, :], g["ident"][0:H, 0:H]).then_inc(carries_up, 1)
            pe.wait_ge(back, 1)
            for m, x in ((1, w), (2, wo)):
                if m == 2:
                    pe.wait_ge(freed, 2)
                for h in range(H):
                    last = nc.tensor.transpose(psz[:, h * P:h * P + NC], x[:, h * P:(h + 1) * P], g["ident"][0:NC, 0:NC])
                last.then_inc(turned, 1)


def gather_sum(nc, g, tag, table, F, H, agg):
    with ExitStack() as ctx:
        def sb(name, shape, dt=F32):
            return ctx.enter_context(nc.sbuf_tensor(f"{tag}s_{name}", shape, dt))

        sem = semaphores(nc, ctx, f"{tag}s_")

        rows = sb("rows", [P, 2, GROUP, D])
        scrap = sb("scrap", [P, 1 + GROUP])
        sel, car = sb("sel", [P, 2, P]), sb("car", [P, 2, P])
        sums = sb("sums", [P, 2, GROUP, AGG_W])
        ix = sb("ix", [P, 2, 2, GROUP], I32)
        ps = [ctx.enter_context(nc.psum_tensor(f"{tag}s_ps{i}", [P, 2, 512], F32)) for i in range(2)]
        cleared, indexed, ready, summed, kept = sem("cleared"), sem("indexed"), sem("ready"), sem("summed"), sem("kept")
        arrived = [[sem(f"arrived{par}{j}") for j in range(GROUP)] for par in range(2)]
        stored = sem("stored")
        block = ctx.enter_context(nc.Block())
        step = F // 2
        KEPT = 2 if H else 1

        @block.gpsimd
        def _(pool):
            nc.gpsimd.memset(rows[:, :, :, :], 0.0).then_inc(cleared, 1)
            nc.gpsimd.memset(sums[:, :, :, :], 0.0).then_inc(cleared, 1)
            nc.gpsimd.memset(ix[:, :, :, :], 0).then_inc(cleared, 1)
            pool.wait_ge(cleared, 3)

            def fetch(turn, par):
                nc.gpsimd.tensor_copy(ix[:, par, 0, :], g["src_i"][:, bass.ds(turn * GROUP, GROUP)]).then_inc(indexed, 1)
                pool.wait_ge(indexed, turn * 2 + 1)
                take_wait(nc, g, scrap[:, 0:1])
                for j in range(GROUP):
                    nc.gpsimd.indirect_dma_start(rows[:, par, j, 0:F], None, table,
                                                 bass.IndirectOffsetOnAxis(ap=ix[:, par, 0, j:j + 1], axis=0),
                                                 bounds_check=N - 1, oob_is_err=False).then_inc(arrived[par][j], 16)

            def body(turn, par, half):
                nc.gpsimd.tensor_copy(ix[:, par, 1, :], g["put_i"][:, bass.ds(turn * GROUP, GROUP)]).then_inc(indexed, 1)
                fetch(turn + 1, 1 - par)
                for j in range(GROUP):
                    pool.wait_ge(kept, (turn * GROUP + (j + 1)) * KEPT)
                    take_wait(nc, g, scrap[:, j + 1:j + 2])
                    nc.gpsimd.indirect_dma_start(agg, bass.IndirectOffsetOnAxis(ap=ix[:, par, 1, j:j + 1], axis=0),
                                                 sums[:, par, j, 0:agg.shape[1]], None,
                                                 bounds_check=N - 1, oob_is_err=False).then_inc(stored, 16)
                pool.wait_ge(stored, turn * (16 * GROUP) + 16 * GROUP)
                for j in range(GROUP):
                    pool.wait_ge(arrived[1 - par][j], half * 16 + (16 if par == 0 else 32))
            fetch(0, 0)
            over_groups(pool, g, body)

        @block.vector
        def _(dve):
            v = nc.vector
            dve.wait_ge(cleared, 3)

            def body(turn, par, half):
                for j in range(GROUP):
                    c = turn * GROUP + j
                    if at_least(c, 2):
                        dve.wait_ge(summed, c - 1)
                    v.scalar_tensor_tensor(sel[:, j % 2, :], g["iota"][:, :], g["seg_end"][:, bass.ds(c, 1)],
                                           g["upper"][:, :], ALU.is_le, ALU.mult).then_inc(ready, 1)
                    v.tensor_scalar(car[:, j % 2, :], g["iota"][:, :], g["carry_end"][:, bass.ds(c, 1)],
                                    g["last_lane"][:, :], ALU.is_le, ALU.mult).then_inc(ready, 1)
                    dve.wait_ge(arrived[par][j], half * 16 + 16)
                    if H:
                        r3 = rows[:, par, j, 0:F].rearrange("p (h f) -> p h f", h=H)
                        al = g["alpha"][:, bass.ds(c, 1), 0:H].rearrange("p c h -> p (c h)")
                        v.tensor_tensor(r3, r3, al.unsqueeze(2).to_broadcast([P, H, F // H]), ALU.mult).then_inc(ready, 1)
                    else:
                        dve.wait_ge(ready, c * 3 + 2)
                        v.tensor_scalar(sel[:, j % 2, :], sel[:, j % 2, :], g["edge_dinv"][:, bass.ds(c, 1)], None,
                                        ALU.mult).then_inc(ready, 1)
            over_groups(dve, g, body)

        @block.tensor
        def _(pe):
            def body(turn, par, half):
                for j in range(GROUP):
                    c = turn * GROUP + j
                    pe.wait_ge(arrived[par][j], half * 16 + 16)
                    pe.wait_ge(ready, c * 3 + 3)
                    carried = at_least(c, 1)
                    if at_least(c, 2):
                        pe.wait_ge(kept, (c - 1) * KEPT)
                    for a in range(2):
                        last = nc.tensor.matmul(ps[j % 2][:, a, 0:step], sel[:, j % 2, :],
                                                rows[:, par, j, a * step:(a + 1) * step], start=True, stop=not carried)
                    if carried:
                        pe.wait_ge(kept, c * KEPT)
                        before = sums[:, par, j - 1, :] if j else sums[:, 1 - par, GROUP - 1, :]
                        for a in range(2):
                            last = nc.tensor.matmul(ps[j % 2][:, a, 0:step], car[:, j % 2, :],
                                                    before[:, a * step:(a + 1) * step], start=False, stop=True)
                    last.then_inc(summed, 1)
            over_groups(pe, g, body)

        @block.scalar
        def _(act):
            act.wait_ge(cleared, 3)

            def body(turn, par, half):
                for j in range(GROUP):
                    c = turn * GROUP + j
                    act.wait_ge(summed, c + 1)
                    nc.scalar.activation(sums[:, par, j, 0:F].rearrange("p (a f) -> p a f", a=2), ps[j % 2][:, :, 0:step],
                                         ACT.Copy).then_inc(kept, 1)
                    if H:
                        own = g["own_w"][:, bass.ds(c, 1), 0:H].rearrange("p c h -> p (c h)")
                        nc.scalar.activation(sums[:, par, j, F:F + H], own, ACT.Copy).then_inc(kept, 1)
            over_groups(act, g, body)


def dense_pass(nc, g, tag, kind, a, out, scores=None, row=None, agg=None, res=None, weights=None, bias=None):
    H = {"project": 4, "attend": 4, "update": 2, "heads": 12, "conv": 0}[kind]
    S = {"project": KC, "attend": KC, "update": KC + 2, "heads": 2 * KC, "conv": KC}[kind]
    C = {"project": D + 8, "attend": 192 + 4}.get(kind, D)
    F = 192 if kind == "update" else D
    norm = kind in ("update", "heads") or (kind == "conv" and res is not None)
    split = kind != "heads"
    loads = []
    if row is not None:
        loads.append(("row", row, F))
    if agg is not None:
        loads.append(("agg", agg, F + H))
    if res is not None and res is not row:
        loads.append(("res", res, D))
    L = len(loads)
    OUT_W = {"project": D + 10, "attend": 197, "update": D + 25}.get(kind, D)
    cut = {"project": D, "attend": 192, "update": D}.get(kind, D)
    n_store = 2 if scores is not None else 1

    with ExitStack() as ctx:
        def sb(name, shape, dt=F32):
            return ctx.enter_context(nc.sbuf_tensor(f"{tag}_{name}", shape, dt))

        sem = semaphores(nc, ctx, f"{tag}_")

        ins = {name: sb(name, [P, UNROLL, w]) for name, _, w in loads}
        XW = {"update": 256}.get(kind, D)
        x = sb("x", [P, 2, XW])
        hi = sb("hi", [P, 2, S, P], F32R if split else F32)
        lo = sb("lo", [P, 2, S, P], F32R) if split else None
        outs = sb("outs", [P, UNROLL, OUT_W])
        y = sb("y", [P, 2, D])
        own_w = sb("own_w", [P, 2, 12])
        scrap = sb("scrap", [P, 1])
        stats, mv = sb("stats", [P, 2, 2, 6]), sb("mv", [P, 2, 2])
        root, rstd, shift = sb("root", [P, 2, 1]), sb("rstd", [P, 2, 1]), sb("shift", [P, 2, 1])
        if kind == "heads":
            w_st = sb("w_st", [P, 2, P])
        else:
            w_st = sb("w_st", [P, S, C])
            w_hi, w_lo = sb("w_hi", [P, S, C], F32R), sb("w_lo", [P, S, C], F32R)
        const = sb("const", [P, C])
        turned_ps = ctx.enter_context(nc.psum_tensor(f"{tag}_turned_ps", [P, -(-S // 4) * 4, P], F32))
        prods = [ctx.enter_context(nc.psum_tensor(f"{tag}_prod{i}", [P, 1 if C <= 512 else 2, 512], F32)) for i in range(2)]
        pieces = [(0, 0, C)] if C <= 512 else [(0, 0, HALF), (1, HALF, C)]

        loaded = [sem(f"loaded{j}") for j in range(UNROLL)]
        stored = [sem(f"stored{j}") for j in range(UNROLL)]
        w_in, w_made, w_const, w_rounded, w_ready = sem("w_in"), sem("w_made"), sem("w_const"), sem("w_rounded"), sem("w_ready")
        w_zero, built, turned, hi_done, split_done = sem("w_zero"), sem("built"), sem("turned"), sem("hi_done"), sem("split_done")
        multiplied, prod_read, polished, out_ready = sem("multiplied"), sem("prod_read"), sem("polished"), sem("out_ready")
        spread, rooted, shifted = sem("spread"), sem("rooted"), sem("shifted")
        prep_self, build_self, end_self = sem("prep_self"), sem("build_self"), sem("end_self")
        marked_up = sem("marked_up")
        block = ctx.enter_context(nc.Block())

        if kind == "project":
            heads_of, att = (4, 192), (a["L0_gnn_a_src1"], a["L0_gnn_a_dst1"])
        elif kind == "attend":
            heads_of, att = (2, 96), (a["L0_gnn_a_src2"], a["L0_gnn_a_dst2"])
        else:
            heads_of, att = None, ()
        if heads_of:
            att_b = sb("att_b", [P, 2, cut])
            scratch = sb("scratch", [P, S, cut])
            b_col = sb("b_col", [P, S])
        if kind == "project":
            g_col = sb("g_col", [P, S])
        if kind == "update":
            b_col = sb("b_col", [P, 2])
            bu_b = sb("bu_b", [P, D])
            w_fc = sb("w_fc", [64, 64])
            att_t = sb("att_t", [64, 2, 12])
            score_v = sb("score_v", [P, 2, D])
            marked = sb("marked", [P, 2, 2, D])
        N_W_IN = {"project": 5, "attend": 4, "update": 7, "heads": 4, "conv": 2}[kind]

        AHEAD = 1 if kind in ("project", "attend") else 0
        storer = {"project": "sync", "attend": "sync", "update": "gpsimd"}.get(kind, "scalar")
        LAG = UNROLL

        def store(eng, t, slot, turn):
            if kind == "update":
                eng.wait_ge(out_ready, t * 2 + 2)
            else:
                eng.wait_ge(polished if kind in ("heads", "conv") else out_ready, t + 1)
            n = rows_of(t)
            eng.dma_start(tile_rows(out, t), outs[0:n, slot, 0:cut]).then_inc(stored[slot], 16)
            if scores is not None:
                eng.dma_start(tile_rows(scores, t), outs[0:n, slot, cut:OUT_W]).then_inc(stored[slot], 16)

        def all_stored(eng):
            for j in range(UNROLL):
                eng.wait_ge(stored[j], 16 * n_store * ((NT - 1 - j) // UNROLL + 1))

        @block.sync
        def _(sp):
            wait_zero = kind in ("update", "heads")
            if wait_zero:
                sp.wait_ge(w_zero, 3 if kind == "update" else 1)

            def load_w(dst, src, scattered=False):
                sp.dma_start(dst, src, allow_slow_non_contiguous=scattered).then_inc(w_in, 16)
            if kind in ("project", "attend", "conv"):
                load_w(w_st[:, :, 0:cut], weights.rearrange("(s p) c -> p s c", p=P))
            if heads_of:
                load_w(att_b[:, 0, :], att[0].rearrange("h c -> (h c)").partition_broadcast(P))
                load_w(att_b[:, 1, :], att[1].rearrange("h c -> (h c)").partition_broadcast(P))
                load_w(b_col[:, :], bias.rearrange("(s p) -> p s", p=P), True)
            if kind == "project":
                load_w(g_col[:, :], a["L0_gnn_norm_g"].rearrange("(s p) -> p s", p=P), True)
            if kind == "update":
                full = D + P
                load_w(w_st[:, 0:KC + 1, :], weights[0:full, :].rearrange("(s p) c -> p s c", p=P))
                load_w(w_st[0:64, KC + 1, :], weights[full:full + 64, :])
                load_w(b_col[:, 0:1], bias[0:P].rearrange("(p o) -> p o", o=1), True)
                load_w(b_col[0:64, 1:2], bias[P:192].rearrange("(p o) -> p o", o=1), True)
                load_w(bu_b[:, :], a["L0_gnn_bu"].partition_broadcast(P))
                load_w(w_fc[:, :], a["L1_gnn_W_fc"])
                with nc.allow_non_contiguous_dma(reason="two small transposed loads"):
                    sp.dma_start(att_t[:, 0, :], a["L1_gnn_attn_l"].rearrange("h e -> e h")).then_inc(w_in, 16)
                    sp.dma_start(att_t[:, 1, :], a["L1_gnn_attn_r"].rearrange("h e -> e h")).then_inc(w_in, 16)
            if kind == "heads":
                with nc.allow_non_contiguous_dma(reason="small transposed loads"):
                    for k, w in enumerate((a["L1_gnn_W_fc"], a["L1_gnn_W_res"])):
                        for q in range(2):
                            sp.dma_start(w_st[64 * q:64 * q + 64, k, 64 * q:64 * q + 64],
                                         w.rearrange("e d -> d e")).then_inc(w_in, 16)
            if kind == "conv":
                load_w(const[:, :], bias.partition_broadcast(P))

            def load(t, slot, turn):
                if at_least(t, UNROLL):
                    sp.wait_ge(built if res is None and kind != "heads" else prod_read, t - UNROLL + 1)
                n = rows_of(t)
                for name, table, w in loads:
                    sp.dma_start(ins[name][0:n, slot, :], tile_rows(table, t)[:, 0:w]).then_inc(loaded[slot], 16)

            def step(t, slot, turn):
                if live(t):
                    load(t, slot, turn)
                b = back(t, slot, turn, LAG)
                if storer == "sync" and at_least(t, LAG) and live(b[0]):
                    store(sp, *b)
            over_tiles(sp, step, LAG if storer == "sync" else 0)
            if storer == "sync":
                all_stored(sp)

        @block.gpsimd
        def _(pool):
            if kind == "update":
                nc.gpsimd.memset(w_st[:, :, :], 0.0).then_inc(w_zero, 1)
                nc.gpsimd.memset(b_col[:, :], 0.0).then_inc(w_zero, 1)
                nc.gpsimd.memset(x[:, :, :], 0.0).then_inc(w_zero, 1)
                pool.wait_ge(w_zero, 3)
                nc.gpsimd.memset(x[:, :, 192:193], 1.0).then_inc(w_zero, 1)
            if kind == "heads":
                nc.gpsimd.memset(w_st[:, :, :], 0.0).then_inc(w_zero, 1)
            if kind == "update":
                pool.wait_ge(w_ready, 1)

                def mark(t, slot, turn):
                    pool.wait_ge(polished, t + 1)
                    if at_least(t, 2):
                        pool.wait_ge(out_ready, t * 2 - 2)
                    for k in range(2):
                        nc.gpsimd.tensor_tensor(marked[:, slot % 2, k, :], outs[:, slot, 0:D], score_v[:, k, :],
                                                ALU.mult).then_inc(marked_up, 1)

                def step(t, slot, turn):
                    if live(t):
                        mark(t, slot, turn)
                    b = back(t, slot, turn, 2)
                    if at_least(t, 2) and live(b[0]):
                        store(pool, *b)
                over_tiles(pool, step, 2)
                all_stored(pool)

        @block.vector
        def _(dve):
            v, n = nc.vector, [0]

            def link(ins_):
                n[0] += 1
                ins_.then_inc(prep_self, 1)
                dve.wait_ge(prep_self, n[0])

            if N_W_IN:
                dve.wait_ge(w_in, 16 * (8 if kind == "update" else N_W_IN))
            if heads_of:
                nh, width = heads_of
                for k in range(2):
                    link(v.tensor_tensor(scratch[:, :, :], w_st[:, :, 0:cut],
                                         att_b[:, k:k + 1, :].to_broadcast([P, S, cut]), ALU.mult))
                    for h in range(nh):
                        link(v.tensor_reduce(w_st[:, :, cut + k * nh + h], scratch[:, :, h * width:(h + 1) * width], AX.X, ALU.add))
                v.tensor_copy(scratch[:, 0, 0:1], b_col[:, 0:1]).then_inc(w_made, 1)
                dve.wait_ge(w_const, 1)
                if len(pieces) == 2:
                    link(v.tensor_copy(const[:, 0:HALF], prods[0][:, 0, 0:HALF]))
                    link(v.tensor_copy(const[:, HALF:C], prods[0][:, 1, 0:C - HALF]))
                else:
                    link(v.tensor_copy(const[:, :], prods[0][:, 0, 0:C]))
                if kind == "project":
                    link(v.tensor_tensor(w_st[:, :, :], w_st[:, :, :], g_col[:, :].unsqueeze(2).to_broadcast([P, S, C]), ALU.mult))
            if kind == "update":
                dve.wait_ge(w_zero, 4)
                dve.wait_ge(w_const, 1)
                cv = const[:, :].rearrange("p (a f) -> p a f", a=2)
                link(v.tensor_tensor(cv, prods[0][:, :, 0:HALF], bu_b[:, :].rearrange("p (a f) -> p a f", a=2), ALU.add))
                link(v.tensor_copy(w_st[64:65, KC + 1, :], const[64:65, :]))
                for k in range(2):
                    link(v.tensor_copy(score_v[:, k, 0:512], turned_ps[:, 0:4, :].rearrange("p s c -> p (s c)") if k == 0
                                       else prods[1][:, 0, :]))
                    link(v.tensor_copy(score_v[:, k, 512:D], turned_ps[:, 4:6, :].rearrange("p s c -> p (s c)") if k == 0
                                       else prods[1][:, 1, 0:D - 512]))
            if kind == "heads":
                v.tensor_copy(const[:, 0:1], w_st[:, 0, 0:1]).then_inc(w_ready, 1)
            else:
                v.tensor_copy(y[:, 0, 0:1], w_st[:, 0, 0:1]).then_inc(w_made, 1)
                dve.wait_ge(w_rounded, 1)
                v.tensor_tensor(w_lo[:, :, :], w_st[:, :, :], w_hi[:, :, :].bitcast(F32), ALU.subtract).then_inc(w_ready, 1)

            bc = Count(build_self, {"project": 2, "attend": 2, "update": 2, "heads": 2, "conv": 1}[kind])
            ec = Count(end_self, 0)
            ec.per = {"project": 2, "attend": 1, "update": 3, "heads": 3, "conv": 4 if norm else 1}[kind]

            def stat(t, s2, src):
                c = bc if kind == "project" else ec
                v.bn_stats(stats[:, s2, 0, :], src[:, 0:HALF]).then_inc(c.sem, 1)
                c.n += 1
                c.link(dve, v.bn_stats(stats[:, s2, 1, :], src[:, HALF:D]))
                v.memset(scrap[:, :], 0.0)
                v.bn_aggr(mv[:, s2, :], stats[:, s2, :, :].rearrange("p a s -> p (a s)")).then_inc(spread, 1)

            def shift_of(t, s2):
                dve.wait_ge(rooted, t + 1)
                v.reciprocal(rstd[:, s2, :], root[:, s2, :]).then_inc(shifted, 1)
                dve.wait_ge(shifted, t * 2 + 1)
                v.scalar_tensor_tensor(shift[:, s2, :], mv[:, s2, 0:1], -1.0, rstd[:, s2, :], ALU.mult, ALU.mult).then_inc(shifted, 1)

            def build(t, slot, turn):
                s2 = slot % 2
                bc.step(t)
                dve.wait_ge(loaded[slot], turn * (16 * L) + 16 * L)
                if kind == "project":
                    stat(t, s2, ins["row"][:, slot, :])
                    if at_least(t, 2):
                        dve.wait_ge(built, t - 1)
                    shift_of(t, s2)
                    return
                if at_least(t, 2):
                    dve.wait_ge(turned, t - 1)
                r, ag = ins["row"][:, slot, :], ins["agg"][:, slot, 0:F]
                if kind == "conv":
                    bc.n += 1
                    v.scalar_tensor_tensor(x[:, s2, :], r, g["own_d"][:, bass.ds(t, 1)], ag, ALU.mult, ALU.add).then_inc(built, 1)
                    return
                extra = g["has_own"][:, bass.ds(t, 1)].to_broadcast([P, H]) if kind == "heads" else g["ones"][:, 0:H]
                bc.link(dve, v.tensor_tensor(own_w[:, s2, 0:H], ins["agg"][:, slot, F:F + H], extra, ALU.add))
                x3 = x[:, s2, 0:F].rearrange("p (h f) -> p h f", h=H)
                bc.link(dve, v.tensor_tensor(x3, r.rearrange("p (h f) -> p h f", h=H),
                                             own_w[:, s2, 0:H].unsqueeze(2).to_broadcast([P, H, F // H]), ALU.mult))
                v.tensor_tensor(x[:, s2, 0:F], x[:, s2, 0:F], ag, ALU.add).then_inc(built, 1)

            def low(t, slot, turn):
                dve.wait_ge(hi_done, t + 1)
                if at_least(t, 2):
                    dve.wait_ge(multiplied, t - 1)
                s2 = slot % 2
                v.tensor_tensor(lo[:, s2, :, :], turned_ps[:, 0:S, :], hi[:, s2, :, :].bitcast(F32), ALU.subtract).then_inc(split_done, 1)

            def end(t, slot, turn):
                s2 = slot % 2
                ec.step(t)
                pr = prods[s2]
                dve.wait_ge(multiplied, t + 1)
                if kind in ("project", "attend"):
                    if at_least(t, UNROLL):
                        dve.wait_ge(stored[slot], turn * (16 * n_store))
                    o = outs[:, slot, :]
                    if kind == "project":
                        ec.link(dve, v.tensor_tensor(o[:, 0:D].rearrange("p (a f) -> p a f", a=2), pr[:, :, 0:HALF],
                                                     const[:, 0:D].rearrange("p (a f) -> p a f", a=2), ALU.add))
                        ec.n += 1
                        v.tensor_tensor(o[:, D:C], pr[:, 1, HALF:C - HALF], const[:, D:C], ALU.add).then_inc(ec.sem, 1)
                        dve.wait_ge(ec.sem, ec.base + ec.n)
                        v.tensor_copy(o[:, C:OUT_W], g["node"][:, bass.ds(t * 2, 2)]).then_inc(out_ready, 1)
                    else:
                        ec.link(dve, v.tensor_tensor(o[:, 0:C], pr[:, 0, 0:C], const[:, :], ALU.add))
                        v.tensor_copy(o[:, C:OUT_W], g["node"][:, bass.ds(t * 2, 1)]).then_inc(out_ready, 1)
                    dve.sem_inc(prod_read, 1)
                    return
                if at_least(t, 2):
                    dve.wait_ge(polished, t - 1)
                ys = y[:, s2, :]
                y3, p3 = ys.rearrange("p (a f) -> p a f", a=2), pr[:, :, 0:HALF]
                if kind == "update":
                    ec.link(dve, v.tensor_tensor(y3, p3, ins["res"][:, slot, :].rearrange("p (a f) -> p a f", a=2), ALU.add))
                elif kind == "heads":
                    ec.link(dve, v.scalar_tensor_tensor(y3, p3, 0.0, ins["row"][:, slot, :].rearrange("p (a f) -> p a f", a=2),
                                                        ALU.max, ALU.add))
                else:
                    c3 = const[:, :].rearrange("p (a f) -> p a f", a=2)
                    if not norm:
                        ec.link(dve, v.scalar_tensor_tensor(y3, p3, g["dinv"][:, bass.ds(t, 1)], c3, ALU.mult, ALU.add))
                        dve.sem_inc(prod_read, 1)
                        dve.sem_inc(spread, 1)
                        return
                    r3 = ins["row" if res is row else "res"][:, slot, :].rearrange("p (a f) -> p a f", a=2)
                    ec.link(dve, v.scalar_tensor_tensor(y3, p3, g["dinv"][:, bass.ds(t, 1)], r3, ALU.mult, ALU.add))
                    ec.link(dve, v.tensor_tensor(ys, ys, const[:, :], ALU.add))
                dve.sem_inc(prod_read, 1)
                stat(t, s2, ys)

            def score(t, slot, turn):
                dve.wait_ge(marked_up, t * 2 + 2)
                v.tensor_reduce(outs[:, slot, D:D + 24], marked[:, slot % 2, :, :].rearrange("p k (h f) -> p (k h) f", h=12),
                                AX.X, ALU.add).then_inc(out_ready, 1)
                v.tensor_copy(outs[:, slot, D + 24:D + 25], g["own"][:, bass.ds(t, 1)]).then_inc(out_ready, 1)

            def step(t, slot, turn):
                b = back(t, slot, turn, -AHEAD)
                if live(b[0]):
                    build(*b)
                b = back(t, slot, turn, 3)
                if norm and at_least(t, 3) and live(b[0]):
                    shift_of(b[0], b[1] % 2)
                b = back(t, slot, turn, 2)
                if at_least(t, 2) and live(b[0]):
                    end(*b)
                if live(t) and split:
                    low(t, slot, turn)
                b = back(t, slot, turn, 4)
                if kind == "update" and at_least(t, 4) and live(b[0]):
                    score(*b)
            if AHEAD:
                build(0, 0, 0)
            over_tiles(dve, step, 4 if kind == "update" else 3 if norm else 2)

        @block.scalar
        def _(act):
            if kind != "heads":
                act.wait_ge(w_made, 2 if heads_of else 1)
                nc.scalar.activation(w_hi[:, :, :], w_st[:, :, :], ACT.Copy).then_inc(w_rounded, 1)

            def root_of(t, s2):
                act.wait_ge(spread, t + 1)
                nc.scalar.activation(root[:, s2, :], mv[:, s2, 1:2], ACT.Sqrt, bias=g["eps"][:, 0:1]).then_inc(rooted, 1)

            def normalise(t, slot, turn):
                s2 = slot % 2
                root_of(t, s2)
                act.wait_ge(shifted, t * 2 + 2)
                if at_least(t, 2):
                    act.wait_ge(turned, t - 1)
                nc.scalar.activation(x[:, s2, :], ins["row"][:, slot, :], ACT.Identity, bias=shift[:, s2, :],
                                     scale=rstd[:, s2, :]).then_inc(built, 1)

            def high(t, slot, turn):
                s2 = slot % 2
                act.wait_ge(turned, t + 1)
                if at_least(t, 2):
                    act.wait_ge(multiplied, t - 1)
                nc.scalar.activation(hi[:, s2, :, :], turned_ps[:, 0:S, :], ACT.Copy).then_inc(hi_done, 1)

            def polish(t, slot, turn):
                s2 = slot % 2
                if norm:
                    act.wait_ge(shifted, t * 2 + 2)
                else:
                    act.wait_ge(spread, t + 1)
                if at_least(t, UNROLL):
                    act.wait_ge(stored[slot], turn * (16 * n_store))
                if norm:
                    nc.scalar.activation(outs[:, slot, 0:D], y[:, s2, :], ACT.Identity, bias=shift[:, s2, :],
                                         scale=rstd[:, s2, :]).then_inc(polished, 1)
                else:
                    nc.scalar.activation(outs[:, slot, 0:D], y[:, s2, :], ACT.Relu).then_inc(polished, 1)

            def step(t, slot, turn):
                b = back(t, slot, turn, -1)
                if kind == "project" and live(b[0]):
                    normalise(*b)
                if live(t):
                    high(t, slot, turn)
                b = back(t, slot, turn, 2)
                if norm and at_least(t, 2) and live(b[0]):
                    root_of(b[0], b[1] % 2)
                b = back(t, slot, turn, 3)
                if kind not in ("project", "attend") and at_least(t, 3) and live(b[0]):
                    polish(*b)
                b = back(t, slot, turn, 4)
                if storer == "scalar" and at_least(t, 4) and live(b[0]):
                    store(act, *b)
            if kind == "project":
                normalise(0, 0, 0)
            over_tiles(act, step, 4)
            if storer == "scalar":
                all_stored(act)

        @block.tensor
        def _(pe):
            if heads_of:
                pe.wait_ge(w_made, 1)
                for bank, c0, c1 in pieces:
                    for k in range(S):
                        last = nc.tensor.matmul(prods[0][:, bank, 0:c1 - c0], b_col[:, k:k + 1].to_broadcast([P, P]),
                                                w_st[:, k, c0:c1], start=(k == 0), stop=(k == S - 1))
                last.then_inc(w_const, 1)
            if kind == "update":
                pe.wait_ge(w_in, 16 * 8)
                pe.wait_ge(w_zero, 4)
                for bank, c0, c1 in pieces:
                    for k in range(2):
                        nc.tensor.matmul(prods[0][:, bank, 0:c1 - c0], b_col[:, k:k + 1].to_broadcast([P, P]),
                                         w_st[:, KC + k, c0:c1], start=(k == 0), stop=(k == 1))
                for k in range(2):
                    for h in range(12):
                        o = turned_ps[:, h // 2, 64 * (h % 2):64 * (h % 2) + 64] if k == 0 else \
                            prods[1][:, h // 8, 64 * (h % 8):64 * (h % 8) + 64]
                        last = nc.tensor.matmul(o, att_t[:, k, h:h + 1].to_broadcast([64, P]), w_fc[:, :], start=True, stop=True)
                last.then_inc(w_const, 1)
            pe.wait_ge(w_ready, 1)

            def turn_over(t, slot, turn):
                pe.wait_ge(built, t + 1)
                if at_least(t, 1):
                    pe.wait_ge(split_done if split else hi_done, t)
                s2 = slot % 2
                for s in range(S):
                    if kind == "update":
                        src = ins["res"][:, slot, s * P:(s + 1) * P] if s < KC else x[:, s2, (s - KC) * P:(s - KC + 1) * P]
                    elif kind == "heads":
                        src = x[:, s2, s * P:(s + 1) * P] if s < KC else ins["row"][:, slot, (s - KC) * P:(s - KC + 1) * P]
                    else:
                        src = x[:, s2, s * P:(s + 1) * P]
                    last = nc.tensor.transpose(turned_ps[:, s, :], src, g["ident"][:, :])
                last.then_inc(turned, 1)

            def multiply(t, slot, turn):
                s2 = slot % 2
                pe.wait_ge(split_done if split else hi_done, t + 1)
                if at_least(t, 2):
                    pe.wait_ge(prod_read, t - 1)
                if kind == "heads":
                    for s in range(KC):
                        o = prods[s2][:, s // 3, (s % 3) * P:(s % 3 + 1) * P]
                        nc.tensor.matmul(o, hi[:, s2, s, :], w_st[:, 0, :], start=True, stop=False)
                        last = nc.tensor.matmul(o, hi[:, s2, KC + s, :], w_st[:, 1, :], start=False, stop=True)
                else:
                    for s in range(S):
                        terms = ((hi, w_hi), (hi, w_lo), (lo, w_hi))
                        for i, (l, w) in enumerate(terms):
                            for bank, c0, c1 in pieces:
                                last = nc.tensor.matmul(prods[s2][:, bank, 0:c1 - c0], l[:, s2, s, :], w[:, s, c0:c1],
                                                        start=(s == 0 and i == 0), stop=(s == S - 1 and i == 2))
                last.then_inc(multiplied, 1)

            def step(t, slot, turn):
                if live(t):
                    turn_over(t, slot, turn)
                b = back(t, slot, turn, 1)
                if at_least(t, 1) and live(b[0]):
                    multiply(*b)
            over_tiles(pe, step, 1)


_OUTS = [((N, D), "float32")]


def kernel(**inputs):
    import numpy as _np
    import concourse.bacc as _bacc
    from concourse import mybir as _mybir
    from concourse.bass_utils import run_bass_kernel_spmd as _run

    nc = _bacc.Bacc("TRN2", target_bir_lowering=False, num_devices=1)
    arrays, args = {}, {}
    for name in inputs:
        arr = _np.ascontiguousarray(inputs[name])
        arrays[f"in_{name}_dram"] = arr
        args[name] = nc.dram_tensor(f"in_{name}_dram", arr.shape, _mybir.dt.from_np(arr.dtype), kind="ExternalInput").ap()
    out = nc.dram_tensor("out_0_dram", _OUTS[0][0], _mybir.dt.float32, kind="ExternalOutput").ap()
    build(nc, args, out)
    r = _run(nc, [arrays], core_ids=[0])
    return r.results[0]["out_0_dram"]
```
